# Optimizing a Trainium2 kernel written in Bass

```python
import numpy as np
import jax
import jax.numpy as jnp

def _softmax(x, axis=-1):
    return jax.nn.softmax(x, axis=axis)

def _gelu(x):
    return jax.nn.gelu(x, approximate=True)

def _silu(x):
    return jax.nn.silu(x)

def _sigmoid(x):
    return jax.nn.sigmoid(x)

def _layernorm(x, axis=-1, eps=1e-05):
    m = jnp.mean(x, axis=axis, keepdims=True)
    v = jnp.var(x, axis=axis, keepdims=True)
    return (x - m) / jnp.sqrt(v + eps)

def _scatter_add(tgt, idx, src, axis=0):
    return tgt.at[idx].add(src)

def _segment_sum(src, seg, n):
    return jax.ops.segment_sum(src, seg, n)
kernel_name = 'mk_prb_d2_jaxref_r2_f0c7f4'

def setup_inputs(seed: int=0):
    np.random.seed(seed)
    _w = jnp.asarray

    def _L0_attn_setup():
        import jax, jax.numpy as jnp
        import numpy as np
        from jax import lax
        D_MODEL = 512
        D_STATE = 16
        BATCH = 8
        SEQ = 1024

        def _silu(x):
            return x * jax.nn.sigmoid(x)

        def _depthwise_conv(x, conv_w):
            xc = jnp.swapaxes(x, 1, 2)
            y = lax.conv_general_dilated(xc, conv_w, window_strides=(1,), padding=[(1, 1)], dimension_numbers=('NCH', 'OIH', 'NCH'), feature_group_count=conv_w.shape[0])
            return jnp.swapaxes(y, 1, 2)

        def _ssm(x, A, B_ssm, C_ssm, D_ssm):
            Abar = jax.nn.sigmoid(A)
            b, l, c = x.shape
            h0 = jnp.zeros((b, c, A.shape[1]), x.dtype)

            def step(h, xt):
                h = h * Abar + xt[..., None] * B_ssm
                y = jnp.einsum('bcs,cs->bc', h, C_ssm) + D_ssm * xt
                return (h, y)
            _, ys = lax.scan(step, h0, jnp.swapaxes(x, 0, 1))
            return jnp.swapaxes(ys, 0, 1)
        key = jax.random.key(seed)
        ks = jax.random.split(key, 12)
        s = 0.02
        return {'x': jax.random.normal(ks[0], (BATCH, SEQ, D_MODEL), jnp.float32), 'w1_w': jax.random.normal(ks[1], (D_MODEL, D_MODEL), jnp.float32) * s, 'w1_b': jnp.zeros((D_MODEL,), jnp.float32), 'v1_w': jax.random.normal(ks[2], (D_MODEL, D_MODEL), jnp.float32) * s, 'v1_b': jnp.zeros((D_MODEL,), jnp.float32), 'w2_w': jax.random.normal(ks[3], (D_MODEL, D_MODEL), jnp.float32) * s, 'w2_b': jnp.zeros((D_MODEL,), jnp.float32), 'conv_w': jax.random.normal(ks[4], (D_MODEL, 1, 3), jnp.float32) * s, 'A': jax.random.normal(ks[5], (D_MODEL, D_STATE), jnp.float32), 'B_ssm': jax.random.normal(ks[6], (D_MODEL, D_STATE), jnp.float32) * s, 'C_ssm': jax.random.normal(ks[7], (D_MODEL, D_STATE), jnp.float32) * s, 'D_ssm': jnp.ones((D_MODEL,), jnp.float32)}
    _L0_attn_in = _L0_attn_setup()

    def _L0_ffn_setup():
        import jax, jax.numpy as jnp
        import numpy as np
        BLOCK_SIZE = 32
        FP6_E2M3_MAX = 7.5

        def _build_fp6_e2m3_grid():
            vals = set()
            for bits in range(64):
                s = bits >> 5 & 1
                e = bits >> 3 & 3
                m = bits & 7
                v = m / 8.0 if e == 0 else (1.0 + m / 8.0) * 2.0 ** (e - 1)
                vals.add(-v if s else v)
            return np.array(sorted(vals), dtype=np.float32)
        _GRID = jnp.asarray(_build_fp6_e2m3_grid())

        def _nearest_on_grid(x, grid):
            idx = jnp.clip(jnp.searchsorted(grid, x), 0, grid.shape[0] - 1)
            idx_lo = jnp.maximum(idx - 1, 0)
            v_hi = grid[idx]
            v_lo = grid[idx_lo]
            return jnp.where(jnp.abs(x - v_lo) <= jnp.abs(x - v_hi), v_lo, v_hi)

        def _mx_quantize(t, eps=1e-30):
            rows, K = t.shape
            blocks = t.reshape(rows, K // BLOCK_SIZE, BLOCK_SIZE)
            scales = jnp.maximum(jnp.max(jnp.abs(blocks), axis=-1) / FP6_E2M3_MAX, eps)
            q = _nearest_on_grid(blocks / scales[..., None], _GRID)
            return (q, scales)
        key = jax.random.key(seed)
        k1, k2, k3 = jax.random.split(key, 3)
        x = jax.random.normal(k1, (8, 4096, 512), dtype=jnp.float32)
        weight = jax.random.normal(k2, (512, 512), dtype=jnp.float32) * 0.02
        bias = jax.random.normal(k3, (512,), dtype=jnp.float32) * 0.02
        return {'x': x, 'weight': weight, 'bias': bias}
    _L0_ffn_in = _L0_ffn_setup()

    def _L1_attn_setup():
        import jax, jax.numpy as jnp
        import numpy as np
        DIM = 512
        H = 16
        HD = DIM // H
        EPS_DENOM = 1e-06
        EPS_LN = 1e-05
        key = jax.random.key(seed)
        ks = jax.random.split(key, 8)
        B, N = (4, 2048)
        s = 1.0 / np.sqrt(DIM)
        return {'x': jax.random.normal(ks[0], (B, N, DIM), dtype=jnp.float32), 'Wq': jax.random.normal(ks[1], (DIM, DIM), dtype=jnp.float32) * s, 'bq': jnp.zeros((DIM,), dtype=jnp.float32), 'Wk': jax.random.normal(ks[2], (DIM, DIM), dtype=jnp.float32) * s, 'bk': jnp.zeros((DIM,), dtype=jnp.float32), 'Wv': jax.random.normal(ks[3], (DIM, DIM), dtype=jnp.float32) * s, 'bv': jnp.zeros((DIM,), dtype=jnp.float32), 'gamma': jnp.ones((DIM,), dtype=jnp.float32), 'beta': jnp.zeros((DIM,), dtype=jnp.float32)}
    _L1_attn_in = _L1_attn_setup()

    def _L1_ffn_setup():
        import jax, jax.numpy as jnp
        import numpy as np
        DIM = 512

        def _reference_tuple_inner(x, W_r, W_k, W_v, mu_r, mu_k):
            B, T, C = x.shape
            x_prev = jnp.concatenate([jnp.zeros((B, 1, C), x.dtype), x[:, :-1, :]], axis=1)
            xr = mu_r * x + (1.0 - mu_r) * x_prev
            xk = mu_k * x + (1.0 - mu_k) * x_prev
            r = jax.nn.sigmoid(jnp.einsum('btc,dc->btd', xr, W_r))
            k = jnp.einsum('btc,dc->btd', xk, W_k)
            k_act = jnp.square(jax.nn.relu(k))
            out = r * jnp.einsum('btc,dc->btd', k_act, W_v)
            new_state = x[:, -1, :]
            return (out, new_state)
        key = jax.random.key(seed)
        ks = jax.random.split(key, 6)
        B, T, C = (8, 1024, DIM)
        x = jax.random.normal(ks[0], (B, T, C), dtype=jnp.float32)
        s = 1.0 / np.sqrt(C)
        W_r = jax.random.uniform(ks[1], (C, C), jnp.float32, -s, s)
        W_k = jax.random.uniform(ks[2], (C, C), jnp.float32, -s, s)
        W_v = jax.random.uniform(ks[3], (C, C), jnp.float32, -s, s)
        mu_r = jax.random.uniform(ks[4], (C,), jnp.float32)
        mu_k = jax.random.uniform(ks[5], (C,), jnp.float32)
        return {'x': x, 'W_r': W_r, 'W_k': W_k, 'W_v': W_v, 'mu_r': mu_r, 'mu_k': mu_k}
    _L1_ffn_in = _L1_ffn_setup()
    _d = {'L0_attn_x': _L0_attn_in['x'], 'L0_attn_w1_w': _L0_attn_in['w1_w'], 'L0_attn_w1_b': _L0_attn_in['w1_b'], 'L0_attn_v1_w': _L0_attn_in['v1_w'], 'L0_attn_v1_b': _L0_attn_in['v1_b'], 'L0_attn_w2_w': _L0_attn_in['w2_w'], 'L0_attn_w2_b': _L0_attn_in['w2_b'], 'L0_attn_conv_w': _L0_attn_in['conv_w'], 'L0_attn_A': _L0_attn_in['A'], 'L0_attn_B_ssm': _L0_attn_in['B_ssm'], 'L0_attn_C_ssm': _L0_attn_in['C_ssm'], 'L0_attn_D_ssm': _L0_attn_in['D_ssm'], 'L0_ffn_weight': _L0_ffn_in['weight'], 'L0_ffn_bias': _L0_ffn_in['bias'], 'L1_attn_Wq': _L1_attn_in['Wq'], 'L1_attn_bq': _L1_attn_in['bq'], 'L1_attn_Wk': _L1_attn_in['Wk'], 'L1_attn_bk': _L1_attn_in['bk'], 'L1_attn_Wv': _L1_attn_in['Wv'], 'L1_attn_bv': _L1_attn_in['bv'], 'L1_attn_gamma': _L1_attn_in['gamma'], 'L1_attn_beta': _L1_attn_in['beta'], 'L1_ffn_W_r': _L1_ffn_in['W_r'], 'L1_ffn_W_k': _L1_ffn_in['W_k'], 'L1_ffn_W_v': _L1_ffn_in['W_v'], 'L1_ffn_mu_r': _L1_ffn_in['mu_r'], 'L1_ffn_mu_k': _L1_ffn_in['mu_k']}
    _x0 = _d['L0_attn_x']
    _d['L0_attn_x'] = jax.random.normal(jax.random.fold_in(jax.random.key(seed), 1), (2, 4096, 512), dtype=_x0.dtype)
    del _x0
    return _d

def reference(L0_attn_x, L0_attn_w1_w, L0_attn_w1_b, L0_attn_v1_w, L0_attn_v1_b, L0_attn_w2_w, L0_attn_w2_b, L0_attn_conv_w, L0_attn_A, L0_attn_B_ssm, L0_attn_C_ssm, L0_attn_D_ssm, L0_ffn_weight, L0_ffn_bias, L1_attn_Wq, L1_attn_bq, L1_attn_Wk, L1_attn_bk, L1_attn_Wv, L1_attn_bv, L1_attn_gamma, L1_attn_beta, L1_ffn_W_r, L1_ffn_W_k, L1_ffn_W_v, L1_ffn_mu_r, L1_ffn_mu_k):

    def _L0_attn_ref(x, w1_w, w1_b, v1_w, v1_b, w2_w, w2_b, conv_w, A, B_ssm, C_ssm, D_ssm):
        import jax, jax.numpy as jnp
        import numpy as np
        from jax import lax
        D_MODEL = 512
        D_STATE = 16
        BATCH = 8
        SEQ = 1024

        def _silu(x):
            return x * jax.nn.sigmoid(x)

        def _depthwise_conv(x, conv_w):
            xc = jnp.swapaxes(x, 1, 2)
            y = lax.conv_general_dilated(xc, conv_w, window_strides=(1,), padding=[(1, 1)], dimension_numbers=('NCH', 'OIH', 'NCH'), feature_group_count=conv_w.shape[0])
            return jnp.swapaxes(y, 1, 2)

        def _ssm(x, A, B_ssm, C_ssm, D_ssm):
            Abar = jax.nn.sigmoid(A)
            b, l, c = x.shape
            h0 = jnp.zeros((b, c, A.shape[1]), x.dtype)

            def step(h, xt):
                h = h * Abar + xt[..., None] * B_ssm
                y = jnp.einsum('bcs,cs->bc', h, C_ssm) + D_ssm * xt
                return (h, y)
            _, ys = lax.scan(step, h0, jnp.swapaxes(x, 0, 1))
            return jnp.swapaxes(ys, 0, 1)
        x1 = x @ w1_w.T + w1_b
        x_conv = _silu(_depthwise_conv(x1, conv_w))
        x_ssm = _ssm(x_conv, A, B_ssm, C_ssm, D_ssm)
        v = _silu(x @ v1_w.T + v1_b)
        return x_ssm * v @ w2_w.T + w2_b

    def _L0_ffn_ref(x, weight, bias):
        import jax, jax.numpy as jnp
        import numpy as np
        BLOCK_SIZE = 32
        FP6_E2M3_MAX = 7.5

        def _build_fp6_e2m3_grid():
            vals = set()
            for bits in range(64):
                s = bits >> 5 & 1
                e = bits >> 3 & 3
                m = bits & 7
                v = m / 8.0 if e == 0 else (1.0 + m / 8.0) * 2.0 ** (e - 1)
                vals.add(-v if s else v)
            return np.array(sorted(vals), dtype=np.float32)
        _GRID = jnp.asarray(_build_fp6_e2m3_grid())

        def _nearest_on_grid(x, grid):
            idx = jnp.clip(jnp.searchsorted(grid, x), 0, grid.shape[0] - 1)
            idx_lo = jnp.maximum(idx - 1, 0)
            v_hi = grid[idx]
            v_lo = grid[idx_lo]
            return jnp.where(jnp.abs(x - v_lo) <= jnp.abs(x - v_hi), v_lo, v_hi)

        def _mx_quantize(t, eps=1e-30):
            rows, K = t.shape
            blocks = t.reshape(rows, K // BLOCK_SIZE, BLOCK_SIZE)
            scales = jnp.maximum(jnp.max(jnp.abs(blocks), axis=-1) / FP6_E2M3_MAX, eps)
            q = _nearest_on_grid(blocks / scales[..., None], _GRID)
            return (q, scales)
        batch_shape = x.shape[:-1]
        in_features = x.shape[-1]
        x2 = x.astype(jnp.float32).reshape(-1, in_features)
        w2 = weight.astype(jnp.float32)
        xq, xs = _mx_quantize(x2)
        wq, ws = _mx_quantize(w2)
        xd = (xq * xs[..., None]).reshape(x2.shape)
        wd = (wq * ws[..., None]).reshape(w2.shape)
        out = xd @ wd.T + bias
        return out.reshape(*batch_shape, -1)

    def _L1_attn_ref(x, Wq, bq, Wk, bk, Wv, bv, gamma, beta):
        import jax, jax.numpy as jnp
        import numpy as np
        DIM = 512
        H = 16
        HD = DIM // H
        EPS_DENOM = 1e-06
        EPS_LN = 1e-05
        B, N, C = x.shape
        q = (x @ Wq.T + bq).reshape(B, N, H, HD)
        k = (x @ Wk.T + bk).reshape(B, N, H, HD)
        v = (x @ Wv.T + bv).reshape(B, N, H, HD)
        q = jax.nn.relu(q)
        k = jax.nn.relu(k)
        kv = jnp.einsum('bnhd,bnhp->bhdp', k, v)
        k_sum = k.sum(axis=1)
        denom = jnp.einsum('bnhd,bhd->bnh', q, k_sum)
        denom = jnp.maximum(denom, EPS_DENOM)[..., None]
        ctx = jnp.einsum('bnhd,bhdp->bnhp', q, kv)
        out = (ctx / denom).reshape(B, N, C)
        y = out + x
        mu = y.mean(axis=-1, keepdims=True)
        var = y.var(axis=-1, keepdims=True)
        return (y - mu) / jnp.sqrt(var + EPS_LN) * gamma + beta

    def _L1_ffn_ref(x, W_r, W_k, W_v, mu_r, mu_k):
        import jax, jax.numpy as jnp
        import numpy as np
        DIM = 512

        def _reference_tuple_inner(x, W_r, W_k, W_v, mu_r, mu_k):
            B, T, C = x.shape
            x_prev = jnp.concatenate([jnp.zeros((B, 1, C), x.dtype), x[:, :-1, :]], axis=1)
            xr = mu_r * x + (1.0 - mu_r) * x_prev
            xk = mu_k * x + (1.0 - mu_k) * x_prev
            r = jax.nn.sigmoid(jnp.einsum('btc,dc->btd', xr, W_r))
            k = jnp.einsum('btc,dc->btd', xk, W_k)
            k_act = jnp.square(jax.nn.relu(k))
            out = r * jnp.einsum('btc,dc->btd', k_act, W_v)
            new_state = x[:, -1, :]
            return (out, new_state)
        return _reference_tuple_inner(x, W_r, W_k, W_v, mu_r, mu_k)[0]
    x = L0_attn_x
    xn = _layernorm(x, axis=-1)
    x = x + _L0_attn_ref(xn, L0_attn_w1_w, L0_attn_w1_b, L0_attn_v1_w, L0_attn_v1_b, L0_attn_w2_w, L0_attn_w2_b, L0_attn_conv_w, L0_attn_A, L0_attn_B_ssm, L0_attn_C_ssm, L0_attn_D_ssm) + _L0_ffn_ref(xn, L0_ffn_weight, L0_ffn_bias)
    xn = _layernorm(x, axis=-1)
    x = x + _L1_attn_ref(xn, L1_attn_Wq, L1_attn_bq, L1_attn_Wk, L1_attn_bk, L1_attn_Wv, L1_attn_bv, L1_attn_gamma, L1_attn_beta) + _L1_ffn_ref(xn, L1_ffn_W_r, L1_ffn_W_k, L1_ffn_W_v, L1_ffn_mu_r, L1_ffn_mu_k)
    return x

_drawn_inputs = setup_inputs


def setup_inputs(seed=0):
    import zlib

    import numpy as np

    out = dict(_drawn_inputs(seed))
    spreads = {'L0_attn_w1_b': (0.0, 0.8),
     'L0_attn_v1_b': (0.0, 0.8),
     'L0_attn_w2_b': (0.0, 0.1),
     'L0_attn_D_ssm': (1.0, 0.6),
     'L1_attn_bq': (0.0, 0.8),
     'L1_attn_bk': (0.0, 0.8),
     'L1_attn_bv': (0.0, 0.1),
     'L1_attn_gamma': (1.0, 0.2),
     'L1_attn_beta': (0.0, 0.1)}
    factors = {'L0_attn_w1_w': 8.0,
     'L0_attn_v1_w': 8.0,
     'L0_attn_w2_w': 8.0,
     'L0_attn_conv_w': 8.0,
     'L0_attn_A': 8.0,
     'L0_attn_B_ssm': 8.0,
     'L0_attn_C_ssm': 8.0,
     'L0_ffn_bias': 2.882,
     'L1_attn_Wq': 6.691,
     'L1_attn_Wk': 5.51,
     'L1_ffn_W_r': 6.676,
     'L1_ffn_mu_r': 8.0,
     'L1_ffn_mu_k': 2.672}
    for name, (base, spread) in spreads.items():
        noise = np.random.default_rng([zlib.crc32(name.encode()), seed]).standard_normal(out[name].shape)
        drawn = base * np.exp(spread * noise) if base else spread * noise
        out[name] = jnp.asarray(drawn.astype(out[name].dtype))
    for name, factor in factors.items():
        out[name] = (out[name] * factor).astype(out[name].dtype)
    return out
```

```python
from contextlib import ExitStack

import concourse.bass as bass
from concourse import mybir

P = 128
F32 = mybir.dt.float32
F32R = mybir.dt.float32r
U32 = mybir.dt.uint32
ALU = mybir.AluOpType
ACT = mybir.ActivationFunctionType
AX = mybir.AxisListType

LN_EPS = 1e-5
QBLOCK = 32
FP6_MAX = 7.5
SCALE_EPS = 1e-30
EXPONENT_BITS = 0x7F800000
ROUND_MAGIC = 1.5 * 2.0 ** 20
HEADS = 16
DENOM_EPS = 1e-6

W1, V1, W2, WQT, WK, WQ, WR, WKF, WVF = range(9)
SPLIT_WEIGHTS = 9

VECTORS = ["L0_attn_w1_b", "L1_attn_bq", "L1_ffn_mu_r", "L1_ffn_mu_k", "L0_attn_D_ssm"]


class Shapes:

    def __init__(self, x):
        self.B, self.S, self.D = x.shape
        self.KT = self.D // P
        self.T = self.B * self.S
        self.NT = self.T // P
        self.GT = 4
        self.GN = self.GT * P
        self.NG = self.T // self.GN
        self.NGB = self.NG // self.B
        self.NTB = self.NT // self.B
        assert self.D == 512 and self.NGB % 2 == 0 and self.T % self.GN == 0


def slot_dmas(g, h):
    return (g - h) * 8


def load_row(eng, tile, vector):
    return eng.dma_start(tile[:, :], vector.rearrange("(o d) -> o d", o=1).broadcast_to(list(tile.shape)))


def wait_reuse(eng, sem, n, lag, per=1):
    if not (isinstance(n, int) and n < lag):
        eng.wait_ge(sem, (n - (lag - 1)) * per)


def split_products(eng, out, lhs, rhs, first, last):
    hi, lo = 0, 1
    eng.matmul(out, lhs[hi], rhs[hi], start=first, stop=False)
    eng.matmul(out, lhs[hi], rhs[lo], start=False, stop=False)
    return eng.matmul(out, lhs[lo], rhs[hi], start=False, stop=last)


def phase_tables(nc, sh, ins, scr, keep, banks):
    KT, D = sh.KT, sh.D
    NS = ins["L0_attn_A"].shape[1]
    GS = KT * NS
    names = ["L0_attn_w1_w", "L0_attn_v1_w", "L0_attn_w2_w", "L0_ffn_weight", "L1_attn_Wk",
             "L1_attn_Wq", "L1_ffn_W_r", "L1_ffn_W_k", "L1_ffn_W_v", "L1_attn_Wv"]
    NW = len(names)
    with ExitStack() as ctx:
        def sb(name, shape, dt=F32):
            return ctx.enter_context(nc.sbuf_tensor(name, shape, dt))

        def sem(name):
            return keep["semaphores"].enter_context(nc.semaphore(name))

        w_nat = [sb(f"w_nat{i}", [P, KT, D]) for i in range(2)]
        w_split = [sb(f"w_split{i}", [P, 2, KT, D], F32R) for i in range(2)]
        q_work = sb("q_work", [P, KT * D])
        q_work2 = sb("q_work2", [P, KT * D])
        q_max = sb("q_max", [P, KT * D // QBLOCK])
        q_scale = sb("q_scale", [P, KT * D // QBLOCK])
        q_inv = sb("q_inv", [P, KT * D // QBLOCK])
        a_in = sb("a_in", [P, KT, NS])
        b_in = sb("b_in", [P, KT, NS])
        c_in = sb("c_in", [P, KT, NS])
        vec_rows = sb("vec_rows", [len(VECTORS) * KT, P])
        cb = sb("cb", [P, KT, NS])
        cb_sum = sb("cb_sum", [P, KT])
        a_exp = sb("a_exp", [P, GS])
        a_den = sb("a_den", [P, GS])
        a_pow = sb("a_pow", [P, 8, GS])
        out_rows = sb("out_rows", [P, GS, P])
        state_cols = sb("state_cols", [P, GS, P])
        kern = sb("kern", [P, KT, 2 * P])
        state_t = sb("state_t", [P, KT, P, NS])
        decay_rows = sb("decay_rows", [D // 8, P])

        ident_set = sem("a_ident_set")
        mask_set = sem("a_mask_set")
        w_in = [sem(f"a_w_in{i}") for i in range(2)]
        q_step = sem("a_q_step")
        t_full = sem("a_t_full")
        hi_done = sem("a_hi_done")
        lo_done = sem("a_lo_done")
        w_out = [sem(f"a_w_out{i}") for i in range(2)]
        small_in = sem("a_small_in")
        vec_in, vec_t, vec_done = sem("a_vec_in"), sem("a_vec_t"), sem("a_vec_done")
        a_exp_done = sem("a_exp_done")
        a_step = sem("a_step")
        r_step = sem("a_r_step")
        st_done = sem("a_st_done")
        dec_stored = sem("a_dec_stored")
        dec_in = sem("a_dec_in")
        dec_t = sem("a_dec_t")
        dec_done = sem("a_dec_done")
        tab_stored = sem("a_tab_stored")

        ident = keep["ident"]
        TB = banks[0:4]
        SBK = banks[4:6]
        DB = banks[6]
        STEPS = P.bit_length() - 1
        TABLE_STEPS = 2 * STEPS + 8
        NSB = GS // 4
        dec_d = scr["decay"]

        def store_weight(sp, n):
            if n < SPLIT_WEIGHTS:
                sp.wait_ge(lo_done, KT * (n + 1))
                sp.dma_start(scr["w"][n], w_split[n % 2][:, :, :, :].bitcast(F32)).then_inc(w_out[n % 2], 16)
            else:
                sp.wait_ge(hi_done, KT * (n + 1))
                sp.dma_start(scr["wv"], w_split[n % 2][:, 0, :, :].bitcast(F32)).then_inc(w_out[n % 2], 16)

        def quantise_weight(dve, w):
            dve.wait_ge(w_in[WQT % 2], 16 * (WQT // 2 + 1))
            flat = w[:, :, :].rearrange("p t k -> p (t k)")
            blocks = flat.rearrange("p (b e) -> p b e", e=QBLOCK)
            NB = q_max.shape[1]
            work = q_work[:, :].rearrange("p (b e) -> p b e", e=QBLOCK)
            nc.vector.tensor_reduce(q_max[:, :], blocks, AX.X, ALU.max, apply_absolute_value=True).then_inc(q_step, 1)
            dve.wait_ge(q_step, 1)
            nc.vector.tensor_scalar(q_scale[:, :], q_max[:, :], 1.0 / FP6_MAX, SCALE_EPS, ALU.mult, ALU.max)\
              .then_inc(q_step, 1)
            dve.wait_ge(q_step, 2)
            nc.vector.reciprocal(q_inv[:, :], q_scale[:, :]).then_inc(q_step, 1)
            dve.wait_ge(q_step, 3)
            nc.vector.tensor_tensor(work, blocks, q_inv[:, :].unsqueeze(2).broadcast_to([P, NB, QBLOCK]), ALU.mult)\
              .then_inc(q_step, 1)
            dve.wait_ge(q_step, 4)
            nc.vector.tensor_scalar(q_work2[:, :].bitcast(U32), q_work[:, :].bitcast(U32), EXPONENT_BITS, None,
                                    ALU.bitwise_and).then_inc(q_step, 1)
            dve.wait_ge(q_step, 5)
            nc.vector.tensor_scalar(q_work2[:, :], q_work2[:, :], 1.0, ROUND_MAGIC, ALU.max, ALU.mult)\
              .then_inc(q_step, 1)
            dve.wait_ge(q_step, 6)
            nc.vector.tensor_tensor(q_work[:, :], q_work[:, :], q_work2[:, :], ALU.add).then_inc(q_step, 1)
            dve.wait_ge(q_step, 7)
            nc.vector.tensor_tensor(q_work[:, :], q_work[:, :], q_work2[:, :], ALU.subtract).then_inc(q_step, 1)
            dve.wait_ge(q_step, 8)
            nc.vector.tensor_tensor(blocks, work, q_scale[:, :].unsqueeze(2).broadcast_to([P, NB, QBLOCK]), ALU.mult)\
              .then_inc(q_step, 1)

        block = ctx.enter_context(nc.Block("tables"))

        @block.sync
        def _(sp):
            for n in range(NW):
                if n >= 2:
                    sp.wait_ge(t_full, KT * (n - 1))
                sp.dma_start(w_nat[n % 2][:, :, :],
                             ins[names[n]].rearrange("(t p) k -> p t k", p=P)).then_inc(w_in[n % 2], 16)
                if n >= 1:
                    store_weight(sp, n - 1)
            store_weight(sp, NW - 1)
            for i in range(2):
                sp.wait_ge(w_out[i], 16 * ((NW - i + 1) // 2))

        @block.gpsimd
        def _(pool):
            nc.gpsimd.memset(ident[:, :], 0.0).then_inc(ident_set, 1)
            pool.wait_ge(ident_set, 1)
            nc.gpsimd.affine_select(out=ident[:, :], in_=ident[:, :], compare_op=ALU.not_equal, fill=1.0,
                                    base=0, pattern=[[-1, P]], channel_multiplier=1).then_inc(ident_set, 1)
            own, carry = keep["own_mask"], keep["carry_mask"]
            NCB = own.shape[2] // sh.B
            nc.gpsimd.memset(own[:, :, :], 1.0).then_inc(mask_set, 1)
            pool.wait_ge(mask_set, 1)
            nc.gpsimd.affine_select(out=own[:, :, :], in_=own[:, :, :], compare_op=ALU.is_ge, fill=0.0, base=0,
                                    pattern=[[-NS, 8], [0, own.shape[2]]], channel_multiplier=1).then_inc(mask_set, 1)
            pool.wait_ge(mask_set, 2)
            nc.gpsimd.affine_select(out=own[:, :, :], in_=own[:, :, :], compare_op=ALU.is_ge, fill=0.0, base=NS - 1,
                                    pattern=[[NS, 8], [0, own.shape[2]]], channel_multiplier=-1).then_inc(mask_set, 1)
            pool.wait_ge(mask_set, 3)
            for b in range(sh.B):
                nc.gpsimd.memset(own[:, :, (b + 1) * NCB - 1:(b + 1) * NCB], 0.0).then_inc(mask_set, 1)
            nc.gpsimd.memset(carry[:, :, :], 1.0).then_inc(mask_set, 1)
            pool.wait_ge(mask_set, 3 + sh.B + 1)
            for b in range(sh.B):
                nc.gpsimd.memset(carry[:, :, b * NCB:b * NCB + 1], 0.0).then_inc(mask_set, 1)
            nc.gpsimd.memset(keep["batch_mask"][:, :], 1.0).then_inc(mask_set, 1)
            pool.wait_ge(mask_set, 3 + 2 * sh.B + 2)
            for b in range(sh.B):
                nc.gpsimd.memset(keep["batch_mask"][:, b * sh.NGB:b * sh.NGB + 1], 0.0).then_inc(mask_set, 1)
            nc.gpsimd.memset(keep["neg_half"][:, :], -0.5).then_inc(mask_set, 1)

            nc.gpsimd.memset(state_cols[:, :, 0:1], 1.0).then_inc(r_step, 1)
            for j in range(STEPS):
                L = 1 << j
                pool.wait_ge(r_step, j + 1)
                pool.wait_ge(a_step, 2 + j)
                nc.gpsimd.tensor_tensor(state_cols[:, :, L:2 * L], state_cols[:, :, 0:L],
                                        a_pow[:, j, :].unsqueeze(2).broadcast_to([P, GS, L]),
                                        ALU.mult).then_inc(r_step, 1)

        @block.scalar
        def _(act):
            for name, tile in (("L0_attn_A", a_in), ("L0_attn_B_ssm", b_in), ("L0_attn_C_ssm", c_in)):
                act.dma_start(tile[:, :, :], ins[name].rearrange("(t p) s -> p t s", p=P)).then_inc(small_in, 16)
            for i, name in enumerate(VECTORS):
                act.dma_start(vec_rows[i * KT:(i + 1) * KT, :],
                              ins[name].rearrange("(t p) -> t p", p=P)).then_inc(vec_in, 16)
            act.dma_start(keep["conv_col"][:, :, :],
                          ins["L0_attn_conv_w"].rearrange("(t p) o k -> p t (o k)", p=P)).then_inc(small_in, 16)
            act.dma_start(keep["bv_row"][:, :], ins["L1_attn_bv"].rearrange("(o d) -> o d", o=1)).then_inc(small_in, 16)
            act.wait_ge(small_in, 16 * 5)
            act.activation(a_exp[:, :], a_in[:, :, :].rearrange("p t s -> p (t s)"), ACT.Exp,
                           scale=-1.0).then_inc(a_exp_done, 1)
            act.wait_ge(vec_t, 1)
            nc.scalar.activation(keep["cols"][:, :], DB[:, 0:len(VECTORS) * KT], ACT.Copy).then_inc(vec_done, 1)
            for n in range(NW):
                for kt in range(KT):
                    act.wait_ge(t_full, KT * n + kt + 1)
                    if n >= 2 and kt == 0:
                        act.wait_ge(w_out[n % 2], 16 * (n // 2))
                    dst = w_split[n % 2][:, 0, kt, :]
                    if n >= SPLIT_WEIGHTS:
                        dst = dst.bitcast(F32)
                    act.activation(dst, TB[kt][:, :], ACT.Copy).then_inc(hi_done, 1)
            for q in range(NSB):
                act.wait_ge(st_done, q + 1)
                act.activation(state_t[:, q * 4 // NS, :, q * 4 % NS:q * 4 % NS + 4].rearrange("p c s -> p s c"),
                               SBK[q % 2][:, :].rearrange("p (s c) -> p s c", s=4), ACT.Copy).then_inc(dec_done, 1)
            act.wait_ge(dec_done, NSB)
            act.dma_start(scr["state_in"].rearrange("o k x -> k o x"),
                          state_t[:, :, :, :].rearrange("p t c s -> p (t c s)").rearrange("p (o x) -> p o x", x=P)
                          ).then_inc(tab_stored, 16)
            act.wait_ge(a_step, TABLE_STEPS)
            act.dma_start(scr["state_out"].rearrange("(t p) s m -> p t s m", p=P),
                          out_rows[:, :, :].rearrange("p (t s) m -> p t s m", t=KT)).then_inc(tab_stored, 16)
            act.dma_start(scr["kern"].rearrange("(t p) j -> p t j", p=P), kern[:, :, :]).then_inc(tab_stored, 16)
            act.dma_start(dec_d.rearrange("(t p) s -> p t s", p=P),
                          a_pow[:, STEPS, :].rearrange("p (t s) -> p t s", t=KT)).then_inc(dec_stored, 16)
            act.wait_ge(dec_stored, 16)
            act.dma_start(decay_rows[:, :], dec_d.rearrange("(o c) s -> o (c s)", c=8)).then_inc(dec_in, 16)
            act.wait_ge(dec_t, 1)
            act.activation(keep["decay_col"][:, :], DB[:, 0:D // 8], ACT.Copy).then_inc(dec_done, 1)
            act.wait_ge(tab_stored, 48)

        @block.tensor
        def _(pe):
            pe.wait_ge(ident_set, 2)
            pe.wait_ge(vec_in, 16 * len(VECTORS))
            pe.transpose(DB[:, 0:len(VECTORS) * KT], vec_rows[:, :],
                         ident[0:len(VECTORS) * KT, 0:len(VECTORS) * KT]).then_inc(vec_t, 1)
            for n in range(NW):
                pe.wait_ge(w_in[n % 2], 16 * (n // 2 + 1))
                if n == WQT:
                    pe.wait_ge(q_step, 9)
                for kt in range(KT):
                    if n:
                        pe.wait_ge(lo_done, KT * (n - 1) + kt + 1)
                    for ot in range(KT):
                        mm = pe.transpose(TB[kt][:, ot * P:(ot + 1) * P], w_nat[n % 2][:, ot, kt * P:(kt + 1) * P],
                                          ident[:, :])
                    mm.then_inc(t_full, 1)
            pe.wait_ge(r_step, STEPS + 1)
            for q in range(NSB):
                if q >= 2:
                    pe.wait_ge(dec_done, q - 1)
                for s in range(4):
                    mm = pe.transpose(SBK[q % 2][:, s * P:(s + 1) * P], state_cols[:, 4 * q + s, :], ident[:, :])
                mm.then_inc(st_done, 1)
            pe.wait_ge(dec_in, 16)
            pe.wait_ge(vec_done, 1)
            pe.transpose(DB[:, 0:D // 8], decay_rows[:, :], ident[0:D // 8, 0:D // 8]).then_inc(dec_t, 1)

        @block.vector
        def _(dve):
            a_count = [0]

            def chain(ins_):
                a_count[0] += 1
                ins_.then_inc(a_step, 1)
                dve.wait_ge(a_step, a_count[0])

            dve.wait_ge(a_exp_done, 1)
            dve.wait_ge(vec_done, 1)
            chain(nc.vector.tensor_scalar(a_den[:, :], a_exp[:, :], 1.0, None, ALU.add))
            chain(nc.vector.reciprocal(a_pow[:, 0, :], a_den[:, :]))
            for j in range(STEPS):
                chain(nc.vector.tensor_tensor(a_pow[:, j + 1, :], a_pow[:, j, :], a_pow[:, j, :], ALU.mult))
            chain(nc.vector.tensor_tensor(cb[:, :, :], c_in[:, :, :], b_in[:, :, :], ALU.mult))
            chain(nc.vector.memset(kern[:, :, :], 0.0))
            chain(nc.vector.tensor_tensor(out_rows[:, :, 0:1], cb[:, :, :].rearrange("p t s -> p (t s)").unsqueeze(2),
                                          a_pow[:, 0, :].unsqueeze(2), ALU.mult))
            for j in range(STEPS):
                L = 1 << j
                chain(nc.vector.tensor_tensor(out_rows[:, :, L:2 * L], out_rows[:, :, 0:L],
                                              a_pow[:, j, :].unsqueeze(2).broadcast_to([P, GS, L]), ALU.mult))
            chain(nc.vector.tensor_reduce(kern[:, :, P:2 * P - 1],
                                          out_rows[:, :, 0:P - 1].rearrange("p (t s) m -> p t m s", t=KT),
                                          AX.X, ALU.add))
            chain(nc.vector.tensor_reduce(cb_sum[:, :], cb[:, :, :], AX.X, ALU.add))
            chain(nc.vector.tensor_tensor(kern[:, :, P - 1:P], cb_sum[:, :].unsqueeze(2), keep["cols"][:, 4 * KT:5 * KT].unsqueeze(2),
                                          ALU.add))
            assert a_count[0] == TABLE_STEPS

            for n in range(NW):
                if n == WQT:
                    quantise_weight(dve, w_nat[n % 2])
                for kt in range(KT if n < SPLIT_WEIGHTS else 0):
                    dve.wait_ge(hi_done, KT * n + kt + 1)
                    if True:
                        nc.vector.tensor_tensor(w_split[n % 2][:, 1, kt, :], TB[kt][:, :],
                                                w_split[n % 2][:, 0, kt, :].bitcast(F32), ALU.subtract)\
                          .then_inc(lo_done, 1)


def phase_project(nc, sh, ins, scr, keep, banks):
    KT, D, GT, GN, NG = sh.KT, sh.D, sh.GT, sh.GN, sh.NG
    x_in = ins["L0_attn_x"].rearrange("b s d -> (b s) d").rearrange("(g t p) d -> g p t d", t=GT, p=P)
    z_out = scr["z"].rearrange("(g t p) d -> g p t d", t=GT, p=P)
    v_out = scr["v"].rearrange("(g t p) d -> g p t d", t=GT, p=P)
    with ExitStack() as ctx:
        def sb(name, shape, dt=F32):
            return ctx.enter_context(nc.sbuf_tensor(name, shape, dt))

        def sem(name):
            return keep["semaphores"].enter_context(nc.semaphore(name))

        w1 = sb("w1", [P, 2, KT, D], F32R)
        v1 = sb("v1", [P, 2, KT, D], F32R)
        xg = [sb(f"b_xg{h}", [P, GT, D]) for h in range(2)]
        xn = sb("b_xn", [P, GT, D])
        xt = [sb(f"b_xt{h}", [P, 2, KT, GN], F32R) for h in range(2)]
        x1 = [sb(f"b_x1{h}", [P, KT, GN + 2]) for h in range(2)]
        conv = sb("b_conv", [P, KT, GN])
        conv_back = sb("b_conv_back", [P, KT, GN])
        zt = [sb(f"b_zt{h}", [P, GT, D]) for h in range(2)]
        vt = [sb(f"b_vt{h}", [P, GT, D]) for h in range(2)]
        stats = sb("b_stats", [P, GT, 6])
        moments = sb("b_moments", [P, GT, 2])
        var_eps = sb("b_var_eps", [P, GT])
        rstd = sb("b_rstd", [P, GT])
        bv1 = sb("b_bv1", [P, D])

        const_in = sem("b_const_in")
        x_in_sem = [sem(f"b_x_in{h}") for h in range(2)]
        st1, st2, st3 = sem("b_st1"), sem("b_st2"), sem("b_st3")
        rstd_done = sem("b_rstd_done")
        xn_done = sem("b_xn_done")
        t_full = sem("b_t_full")
        hi_done, lo_done = sem("b_hi_done"), sem("b_lo_done")
        x1_full, x1_done = sem("b_x1_full"), sem("b_x1_done")
        halo = sem("b_halo")
        mid_done, left_done, conv_done = sem("b_mid_done"), sem("b_left_done"), sem("b_conv_done")
        v_full, v_sum, v_done = sem("b_v_full"), sem("b_v_sum"), sem("b_v_done")
        z_full, z_done = sem("b_z_full"), sem("b_z_done")
        z_stored = [sem(f"b_z_stored{h}") for h in range(2)]
        v_stored = [sem(f"b_v_stored{h}") for h in range(2)]

        TB, XB, VB, ZB = banks[0:2], banks[2:4], banks[4:6], banks[6:8]
        ident = keep["ident"]
        block = ctx.enter_context(nc.Block("project"))

        def over_groups(eng, body):
            body(0, 0, True, False)
            body(1, 1, False, False)
            if NG > 4:
                with eng.Fori(1, NG // 2 - 1) as i:
                    body(i * 2, 0, False, False)
                    body(i * 2 + 1, 1, False, False)
            body(NG - 2, 0, False, False)
            body(NG - 1, 1, False, True)

        @block.sync
        def _(sp):
            sp.dma_start(xg[0][:, :, :], x_in[0]).then_inc(x_in_sem[0], 16)
            sp.dma_start(w1[:, :, :, :].bitcast(F32), scr["w"][W1]).then_inc(const_in, 16)
            sp.dma_start(v1[:, :, :, :].bitcast(F32), scr["w"][V1]).then_inc(const_in, 16)

            def store_z(g, h):
                sp.wait_ge(z_done, GT * (g + 1))
                sp.dma_start(z_out[g], zt[h][:, :, :]).then_inc(z_stored[h], 16)

            def body(g, h, first, last):
                if not last:
                    if not first:
                        sp.wait_ge(xn_done, GT * g)
                    sp.dma_start(xg[1 - h][:, :, :], x_in[g + 1]).then_inc(x_in_sem[1 - h], 16)
                if not first:
                    store_z(g - 1, 1 - h)
                sp.wait_ge(v_done, GT * (g + 1))
                sp.dma_start(v_out[g], vt[h][:, :, :]).then_inc(v_stored[h], 16)

            over_groups(sp, body)
            store_z(NG - 1, 1)
            for h in range(2):
                sp.wait_ge(z_stored[h], 16 * NG // 2)
                sp.wait_ge(v_stored[h], 16 * NG // 2)

        @block.gpsimd
        def _(pool):
            def rstd_of(g):
                pool.wait_ge(st3, g + 1)
                nc.gpsimd.tensor_tensor(rstd[:, :], var_eps[:, :], keep["neg_half"][:, 0:GT], ALU.pow)\
                  .then_inc(rstd_done, 1)

            with pool.Fori(0, NG) as g:
                rstd_of(g)

        @block.vector
        def _(dve):
            def normalise(g, h):
                dve.wait_ge(x_in_sem[h], slot_dmas(g, h) + 16)
                for t in range(GT):
                    ins_ = nc.vector.bn_stats(stats[:, t, :], xg[h][:, t, :])
                ins_.then_inc(st1, 1)
                dve.wait_ge(st1, g + 1)
                nc.vector.memset(keep["beat"][:, :], 0.0)
                for t in range(GT):
                    ins_ = nc.vector.bn_aggr(moments[:, t, :], stats[:, t, :])
                ins_.then_inc(st2, 1)
                dve.wait_ge(st2, g + 1)
                nc.vector.tensor_scalar(var_eps[:, :], moments[:, :, 1], LN_EPS, None, ALU.add).then_inc(st3, 1)
                nc.vector.tensor_copy(keep["mean0"][:, bass.ds(g * GT, GT)], moments[:, :, 0])
                dve.wait_ge(rstd_done, g + 1)
                nc.vector.tensor_copy(keep["rstd0"][:, bass.ds(g * GT, GT)], rstd[:, :])
                if not (isinstance(g, int) and g == 0):
                    dve.wait_ge(t_full, KT * g)
                for t in range(GT):
                    ins_ = nc.vector.tensor_scalar(xn[:, t, :], xg[h][:, t, :], moments[:, t, 0:1], rstd[:, t:t + 1],
                                                   ALU.subtract, ALU.mult)
                    ins_.then_inc(xn_done, 1)

            def low_part(g, h, kt):
                dve.wait_ge(hi_done, KT * g + kt + 1)
                nc.vector.tensor_tensor(xt[h][:, 1, kt, :], TB[kt % 2][:, :], xt[h][:, 0, kt, :].bitcast(F32),
                                        ALU.subtract).then_inc(lo_done, 1)

            def convolve(g, h):
                src = x1[h]
                for m in range(KT):
                    dve.wait_ge(mid_done, KT * g + m + 1)
                    nc.vector.scalar_tensor_tensor(conv[:, m, :], src[:, m, 0:GN], keep["conv_col"][:, m, 0:1],
                                                   conv[:, m, :], ALU.mult, ALU.add).then_inc(left_done, 1)
                for m in range(KT):
                    dve.wait_ge(left_done, KT * g + m + 1)
                    back = bass.AP(conv_back[:, :, :].tensor, m * GN + P - 1, [[KT * GN, P], [P, GT], [-1, P]])
                    nc.vector.scalar_tensor_tensor(back, src[:, m, 2:GN + 2].rearrange("p (t k) -> p t k", k=P),
                                                   keep["conv_col"][:, m, 2:3],
                                                   conv[:, m, :].rearrange("p (t k) -> p t k", k=P),
                                                   ALU.mult, ALU.add).then_inc(conv_done, 1)

            def body(g, h, first, last):
                if not last:
                    normalise(g + 1, 1 - h)
                dve.wait_ge(x1_done, KT * (g + 1))
                if not first:
                    gate = keep["batch_mask"][:, bass.ds(g, 1)]
                    nc.vector.tensor_scalar(x1[h][:, :, 0:1], x1[1 - h][:, :, GN:GN + 1], gate, None,
                                            ALU.mult).then_inc(halo, 1)
                    nc.vector.tensor_scalar(x1[1 - h][:, :, GN + 1:GN + 2], x1[h][:, :, 1:2], gate, None,
                                            ALU.mult).then_inc(halo, 1)
                    dve.wait_ge(halo, 2 * g + 1)
                    convolve(g - 1, 1 - h)
                for t in range(GT):
                    dve.wait_ge(v_full, GT * g + t + 1)
                    if not (first or (isinstance(g, int) and g == 1)) and t == 0:
                        dve.wait_ge(v_stored[h], slot_dmas(g, h))
                    nc.vector.tensor_tensor(vt[h][:, t, :], VB[t % 2][:, :], bv1[:, :], ALU.add)\
                      .then_inc(v_sum, 1)
                    if not last:
                        low_part(g + 1, 1 - h, t)

            nc.vector.memset(x1[0][:, :, 0:1], 0.0).then_inc(halo, 1)
            nc.vector.memset(x1[1][:, :, GN + 1:GN + 2], 0.0)
            normalise(0, 0)
            for kt in range(KT):
                low_part(0, 0, kt)
            dve.wait_ge(const_in, 16 * 3)
            over_groups(dve, body)
            nc.vector.memset(x1[1][:, :, GN + 1:GN + 2], 0.0).then_inc(halo, 1)
            dve.wait_ge(halo, 2 * NG)
            convolve(NG - 1, 1)

        @block.scalar
        def _(act):
            load_row(act, bv1, ins["L0_attn_v1_b"]).then_inc(const_in, 16)

            def high_part(g, h, kt):
                act.wait_ge(t_full, KT * g + kt + 1)
                nc.scalar.activation(xt[h][:, 0, kt, :], TB[kt % 2][:, :], ACT.Copy).then_inc(hi_done, 1)

            def middle(g, h, m):
                if not (isinstance(g, int) and g == 0):
                    act.wait_ge(z_full, GT * g)
                nc.scalar.activation(conv[:, m, :], x1[h][:, m, 1:GN + 1], ACT.Copy,
                                     scale=keep["conv_col"][:, m, 1:2]).then_inc(mid_done, 1)

            def silu_z(g, h, t):
                act.wait_ge(z_full, GT * g + t + 1)
                if t == 0 and not (isinstance(g, int) and g < 2):
                    act.wait_ge(z_stored[h], slot_dmas(g, h))
                nc.scalar.activation(zt[h][:, t, :], ZB[t % 2][:, :], ACT.Silu).then_inc(z_done, 1)

            def body(g, h, first, last):
                for m in range(KT):
                    act.wait_ge(x1_full, KT * g + m + 1)
                    if m == 0 and not (isinstance(g, int) and g < 2):
                        act.wait_ge(conv_done, KT * (g - 1))
                    nc.scalar.activation(x1[h][:, m, 1:GN + 1], XB[m % 2][:, :], ACT.Identity,
                                         bias=keep["b1_col"][:, m:m + 1]).then_inc(x1_done, 1)
                    if not first:
                        if m == 0:
                            act.wait_ge(x1_done, KT * g)
                        middle(g - 1, 1 - h, m)
                for t in range(GT):
                    if not last:
                        high_part(g + 1, 1 - h, t)
                    act.wait_ge(v_sum, GT * g + t + 1)
                    nc.scalar.activation(vt[h][:, t, :], vt[h][:, t, :], ACT.Silu).then_inc(v_done, 1)
                    if not first:
                        silu_z(g - 1, 1 - h, t)

            for kt in range(KT):
                high_part(0, 0, kt)
            over_groups(act, body)
            act.wait_ge(x1_done, KT * NG)
            for m in range(KT):
                middle(NG - 1, 1, m)
            for t in range(GT):
                silu_z(NG - 1, 1, t)

        @block.tensor
        def _(pe):
            def turn_x(g, kt):
                if kt == 0:
                    pe.wait_ge(xn_done, GT * (g + 1))
                if not (isinstance(g, int) and g == 0 and kt < 2):
                    pe.wait_ge(lo_done, KT * g + kt - 1)
                for t in range(GT):
                    mm = pe.transpose(TB[kt % 2][:, t * P:(t + 1) * P], xn[:, t, kt * P:(kt + 1) * P], ident[:, :])
                mm.then_inc(t_full, 1)

            def turn_z(g, t):
                if t == 0:
                    pe.wait_ge(conv_done, KT * (g + 1))
                if not (isinstance(g, int) and g == 0 and t < 2):
                    pe.wait_ge(z_done, GT * g + t - 1)
                for m in range(KT):
                    mm = pe.transpose(ZB[t % 2][:, m * P:(m + 1) * P], conv_back[:, m, t * P:(t + 1) * P], ident[:, :])
                mm.then_inc(z_full, 1)

            def body(g, h, first, last):
                for m in range(KT):
                    if not (first and m < 2):
                        pe.wait_ge(x1_done, KT * g + m - 1)
                    for kt in range(KT):
                        if m == 0:
                            pe.wait_ge(lo_done, KT * g + kt + 1)
                        mm = split_products(pe, XB[m % 2][:, :],
                                            [w1[:, j, kt, m * P:(m + 1) * P] for j in range(2)],
                                            [xt[h][:, j, kt, :] for j in range(2)], kt == 0, kt == KT - 1)
                    mm.then_inc(x1_full, 1)
                for t in range(GT):
                    if not (first and t < 2):
                        pe.wait_ge(v_sum, GT * g + t - 1)
                    for kt in range(KT):
                        mm = split_products(pe, VB[t % 2][:, :],
                                            [xt[h][:, j, kt, t * P:(t + 1) * P] for j in range(2)],
                                            [v1[:, j, kt, :] for j in range(2)], kt == 0, kt == KT - 1)
                    mm.then_inc(v_full, 1)
                    if not last:
                        turn_x(g + 1, t)
                    if not first:
                        turn_z(g - 1, t)

            for kt in range(KT):
                turn_x(0, kt)
            pe.wait_ge(const_in, 16 * 3)
            over_groups(pe, body)
            for t in range(GT):
                turn_z(NG - 1, t)


def phase_state_space(nc, sh, ins, scr, keep, banks):
    D, T = sh.D, sh.T
    NCH = sh.NT
    OC = 8
    NO = P // OC
    NC = D // P
    U = 4
    COLS = OC * NCH
    z_in = scr["z"].rearrange("(n m) d -> m n d", m=P)
    v_in = scr["v"].rearrange("(n m) d -> m n d", m=P)
    u_out = scr["u"].rearrange("(n m) d -> m n d", m=P)
    kern = scr["kern"]
    with ExitStack() as ctx:
        def sb(name, shape, dt=F32):
            return ctx.enter_context(nc.sbuf_tensor(name, shape, dt))

        def sem(name):
            return keep["semaphores"].enter_context(nc.semaphore(name))

        zg = [sb(f"c_zg{i}", [P, NCH, P]) for i in range(2)]
        vg = [sb(f"c_vg{i}", [P, NCH, P]) for i in range(2)]
        toep = [sb(f"c_toep{i}", [P, OC, P]) for i in range(U)]
        into = [sb(f"c_into{i}", [P, P]) for i in range(U)]
        outof = [sb(f"c_outof{i}", [P, P]) for i in range(U)]
        own_sum = [sb(f"c_own_sum{i}", [P, COLS + 1]) for i in range(2)]
        decay = [sb(f"c_decay{i}", [P, COLS]) for i in range(2)]
        state = [sb(f"c_state{i}", [P, COLS]) for i in range(2)]

        z_in_sem = [sem(f"c_z_in{i}") for i in range(2)]
        v_in_sem = [sem(f"c_v_in{i}") for i in range(2)]
        stream_in = [sem(f"c_stream_in{i}") for i in range(U)]
        s_full, s_done = sem("c_s_full"), sem("c_s_done")
        decay_done, state_done = sem("c_decay_done"), sem("c_state_done")
        y_full, u_done = sem("c_y_full"), sem("c_u_done")
        u_stored = [sem(f"c_u_stored{i}") for i in range(2)]
        zeroed = sem("c_zeroed")
        SB, YB = banks[0:2], banks[2:4]
        own = keep["own_mask"][:, :, :].rearrange("p c n -> p (c n)")
        carry = keep["carry_mask"][:, :, :].rearrange("p c n -> p (c n)")
        block = ctx.enter_context(nc.Block("state_space"))

        def over_octets(eng, body):
            for cg in range(NC):
                if cg == 0:
                    for u in range(U):
                        body(0, 0, u, False)
                with eng.Fori(1 if cg == 0 else 0, NO // U - 1) as i:
                    for u in range(U):
                        body(cg, i * U, u, False)
                for u in range(U):
                    body(cg, NO - U, u, u == U - 1)

        @block.sync
        def _(sp):
            def load_stream(cg, j, u, after):
                o = j + (cg * NO + u)
                if after:
                    sp.wait_ge(y_full, o - U + 1)
                rows = bass.AP(kern.tensor, o * (OC * 2 * P), [[1, P], [2 * P, OC], [1, P]])
                sp.dma_start(toep[u][:, :, :], rows).then_inc(stream_in[u], 16)
                sp.dma_start(into[u][:, :], scr["state_in"][bass.ds(o, 1), :, :].rearrange("o k x -> k (o x)"))\
                  .then_inc(stream_in[u], 16)
                sp.dma_start(outof[u][:, :],
                             scr["state_out_rows"][bass.ds(o, 1), :, :].rearrange("o x m -> x (o m)"))\
                  .then_inc(stream_in[u], 16)

            def load_group(cg, src, tiles, sems, n=1):
                sp.dma_start(tiles[cg % 2][:, :, :], src[:, :, cg * P:(cg + 1) * P]).then_inc(sems[cg % 2], 16)

            load_group(0, z_in, zg, z_in_sem)
            for cg in range(NC):
                for q in range(NO // U):
                    if q == 0:
                        for u in range(U):
                            load_stream(cg, 0, u, cg > 0)
                        if cg == 0:
                            load_group(0, v_in, vg, v_in_sem)
                            load_group(1, z_in, zg, z_in_sem)
                            load_group(1, v_in, vg, v_in_sem)
                    else:
                        for u in range(U):
                            load_stream(cg, q * U, u, True)
                    if cg >= 1 and q == 1:
                        sp.wait_ge(u_done, cg * NO)
                        sp.dma_start(u_out[:, :, (cg - 1) * P:cg * P], vg[(cg - 1) % 2][:, :, :])\
                          .then_inc(u_stored[(cg - 1) % 2], 16)
                        if cg + 1 < NC:
                            load_group(cg + 1, z_in, zg, z_in_sem)
                    if cg >= 1 and q == 2 and cg + 1 < NC:
                        sp.wait_ge(u_stored[(cg - 1) % 2], 16 * ((cg - 1) // 2 + 1))
                        load_group(cg + 1, v_in, vg, v_in_sem)
            sp.wait_ge(u_done, NC * NO)
            sp.dma_start(u_out[:, :, (NC - 1) * P:NC * P], vg[(NC - 1) % 2][:, :, :])\
              .then_inc(u_stored[(NC - 1) % 2], 16)
            for i in range(2):
                sp.wait_ge(u_stored[i], 16 * NC // 2)

        @block.scalar
        def _(act):
            def body(cg, j, u, last):
                o = j + (cg * NO + u)
                if not (cg == 0 and isinstance(o, int) and o < 2):
                    act.wait_ge(state_done, o - 1)
                nc.scalar.activation(decay[u % 2][:, :], carry, ACT.Copy,
                                     scale=keep["decay_col"][:, bass.ds(o, 1)]).then_inc(decay_done, 1)

            body(0, 0, 0, False)
            body(0, 0, 1, False)
            for u in (2, 3):
                body(0, 0, u, False)
            with act.Fori(1, NC * NO // U) as i:
                for u in range(U):
                    body(0, i * U, u, False)

        @block.vector
        def _(dve):
            def states(cg, j, u):
                o = j + (cg * NO + u)
                dve.wait_ge(s_full, o + 1)
                if not (isinstance(o, int) and o < 2):
                    dve.wait_ge(y_full, o - 1)
                nc.vector.tensor_tensor(own_sum[u % 2][:, 1:COLS + 1], SB[u % 2][:, 0:COLS], own, ALU.mult)\
                  .then_inc(s_done, 1)
                dve.wait_ge(s_done, o + 1)
                dve.wait_ge(decay_done, o + 1)
                nc.vector.tensor_tensor_scan(state[u % 2][:, :], decay[u % 2][:, :], own_sum[u % 2][:, 0:COLS],
                                             0.0, ALU.mult, ALU.add).then_inc(state_done, 1)

            def body(cg, j, u, last):
                if u + 1 < U:
                    states(cg, j, u + 1)
                elif not last:
                    states(cg, j + U, 0)
                elif cg + 1 < NC:
                    states(cg + 1, 0, 0)
                o = j + (cg * NO + u)
                if u == 0:
                    dve.wait_ge(v_in_sem[cg % 2], 16 * (cg // 2 + 1))
                dve.wait_ge(y_full, o + 1)
                mine = vg[cg % 2][:, :, bass.ds(j * OC + u * OC, OC)].rearrange("p n c -> p c n")
                nc.vector.tensor_tensor(mine, YB[u % 2][:, 0:COLS].rearrange("p (c n) -> p c n", c=OC), mine,
                                        ALU.mult).then_inc(u_done, 1)

            for i in range(2):
                ins_ = nc.vector.memset(own_sum[i][:, 0:1], 0.0)
            ins_.then_inc(zeroed, 1)
            dve.wait_ge(zeroed, 1)
            states(0, 0, 0)
            over_octets(dve, body)

        @block.tensor
        def _(pe):
            def states(cg, j, u):
                o = j + (cg * NO + u)
                pe.wait_ge(stream_in[u], 48 * (cg * (NO // U)) + (j * (48 // U)) + 48)
                if not (isinstance(o, int) and o < 2):
                    pe.wait_ge(s_done, o - 1)
                zs = zg[cg % 2][:, :, bass.ds(j * OC + u * OC, OC)].rearrange("p n c -> p c n")
                pe.matmul(SB[u % 2][:, 0:COLS].rearrange("p (c n) -> p c n", c=OC), into[u][:, :], zs,
                          start=True, stop=True).then_inc(s_full, 1)

            def body(cg, j, u, last):
                if u + 1 < U:
                    states(cg, j, u + 1)
                elif not last:
                    states(cg, j + U, 0)
                elif cg + 1 < NC:
                    pe.wait_ge(z_in_sem[(cg + 1) % 2], 16 * ((cg + 1) // 2 + 1))
                    states(cg + 1, 0, 0)
                o = j + (cg * NO + u)
                if not (isinstance(o, int) and o < 2):
                    pe.wait_ge(u_done, o - 1)
                for c in range(OC):
                    zc = zg[cg % 2][:, :, bass.ds(j * OC + (u * OC + c), 1)].rearrange("p n c -> p (n c)")
                    pe.matmul(YB[u % 2][:, c * NCH:(c + 1) * NCH], toep[u][:, c, :], zc,
                              start=(c == 0), stop=False, skip_group_check=True)
                pe.wait_ge(state_done, o + 1)
                pe.matmul(YB[u % 2][:, 0:COLS], outof[u][:, :], state[u % 2][:, :], start=False, stop=True,
                          skip_group_check=True).then_inc(y_full, 1)

            pe.wait_ge(z_in_sem[0], 16)
            states(0, 0, 0)
            over_octets(pe, body)


def phase_mix(nc, sh, ins, scr, keep, banks):
    KT, D, NTB, B = sh.KT, sh.D, sh.NTB, sh.B
    NBL = D // QBLOCK
    Q = 4
    assert NTB % Q == 0 and NTB >= 2 * Q
    x_in = ins["L0_attn_x"].rearrange("b s d -> (b s) d").rearrange("(n p) d -> p n d", p=P)
    u_in = scr["u"].rearrange("(n p) d -> p n d", p=P)
    x2_out = scr["x2"].rearrange("(n p) d -> p n d", p=P)
    with ExitStack() as ctx:
        def sb(name, shape, dt=F32):
            return ctx.enter_context(nc.sbuf_tensor(name, shape, dt))

        def sem(name):
            return keep["semaphores"].enter_context(nc.semaphore(name))

        w2 = sb("d_w2", [P, 2, KT, D], F32R)
        wf = sb("d_wf", [P, 2, KT, D], F32R)
        wk = sb("d_wk", [P, 2, KT, D], F32R)
        wv = sb("d_wv", [P, KT, D])
        xs = [sb(f"d_x{i}", [P, D]) for i in range(Q)]
        us = [sb(f"d_u{i}", [P, D]) for i in range(Q)]
        xb = [sb(f"d_xb{i}", [P, D]) for i in range(Q)]
        x2 = [sb(f"d_x2{i}", [P, D]) for i in range(Q)]
        xq = [sb(f"d_xq{i}", [P, D]) for i in range(2)]
        magic = sb("d_magic", [P, 2, D])
        q_max = sb("d_q_max", [P, NBL])
        q_inv = sb("d_q_inv", [P, NBL])
        q_scale = sb("d_q_scale", [P, 2, NBL])
        ut = [sb(f"d_ut{i}", [P, 2, KT, P], F32R) for i in range(2)]
        qt = [sb(f"d_qt{i}", [P, 2, KT, P], F32R) for i in range(2)]
        nt = [sb(f"d_nt{i}", [P, 2, KT, P], F32R) for i in range(2)]
        xn = [sb(f"d_xn{i}", [P, D]) for i in range(2)]
        nat = [sb(f"d_nat{i}", [P, 2, D], F32R) for i in range(Q)]
        kb = sb("d_kb", [P, D])
        kr = [sb(f"d_kr{i}", [P, D]) for i in range(2)]
        kh = [sb(f"d_kh{i}", [P, 2, D], F32R) for i in range(2)]
        kacc = sb("d_kacc", [P, D])
        stats = sb("d_stats", [P, 6])
        moments = [sb(f"d_moments{i}", [P, 2]) for i in range(2)]
        var_eps = sb("d_var_eps", [P, 1])
        rstd = [sb(f"d_rstd{i}", [P, 1]) for i in range(2)]
        res_bias = sb("d_res_bias", [P, D])
        ffn_bias = sb("d_ffn_bias", [P, D])
        bk = sb("d_bk", [P, D])
        zeros = sb("d_zeros", [P, D], F32R)
        ones = sb("d_ones", [P, 1])
        gt = sb("d_gt", [P, KT, D])
        ksum_row = sb("d_ksum_row", [1, D])

        const_in = sem("d_const_in")
        bias_done = sem("d_bias_done")
        set_done = sem("d_set_done")
        x_ld = [sem(f"d_x_ld{i}") for i in range(Q)]
        u_ld = [sem(f"d_u_ld{i}") for i in range(Q)]
        x2_st = [sem(f"d_x2_st{i}") for i in range(Q)]
        prep = sem("d_prep")
        q_sub, q_done = sem("d_q_sub"), sem("d_q_done")
        xb_done = sem("d_xb_done")
        u_full, u_hi, u_lo = sem("d_u_full"), sem("d_u_hi"), sem("d_u_lo")
        q_full, q_hi, q_lo = sem("d_q_full"), sem("d_q_hi"), sem("d_q_lo")
        n_full, n_hi, n_lo = sem("d_n_full"), sem("d_n_hi"), sem("d_n_lo")
        x2_full, x2_done = sem("d_x2_full"), sem("d_x2_done")
        st1, st2, st3 = sem("d_st1"), sem("d_st2"), sem("d_st3")
        rstd_done = sem("d_rstd_done")
        xn_done = sem("d_xn_done")
        nat_hi, nat_lo = sem("d_nat_hi"), sem("d_nat_lo")
        k_full, kb_done = sem("d_k_full"), sem("d_kb_done")
        kr_done, k_hi, k_lo = sem("d_kr_done"), sem("d_k_hi"), sem("d_k_lo")
        kacc_done = sem("d_kacc_done")
        g_full, g_done = sem("d_g_full"), sem("d_g_done")
        ks_full, ks_done = sem("d_ks_full"), sem("d_ks_done")
        kv_full, kv_done = sem("d_kv_full"), sem("d_kv_done")

        BA, BB, BX, BK = banks[0:4]
        BG = banks[4:8]
        ident = keep["ident"]
        PREP = 8
        block = ctx.enter_context(nc.Block("mix"))

        def over_steps(eng, b, step):
            def one(n, q):
                known = isinstance(n, int)
                step(b, n, b * NTB + n, q,
                     one=not known or n < NTB,
                     two=not known or 1 <= n <= NTB,
                     three=not known or 2 <= n <= NTB + 1,
                     turn=not known or n + 1 < NTB,
                     prepare=not known or n + 2 < NTB,
                     load=not known or n + Q < NTB)

            for n in range(Q):
                one(n, n)
            if NTB > 2 * Q:
                with eng.Fori(1, NTB // Q - 1) as i:
                    for q in range(Q):
                        one(i * Q + q, q)
            for n in range(NTB - Q, NTB + 2):
                one(n, n % Q)

        @block.sync
        def _(sp):
            def load(N, q):
                if not (isinstance(N, int) and N < Q):
                    used = N - (Q - 1)
                    sp.wait_ge(prep, used * PREP)
                    sp.wait_ge(xb_done, used)
                sp.dma_start(xs[q][:, :], x_in[:, bass.ds(N, 1), :].rearrange("p n d -> p (n d)"))\
                  .then_inc(x_ld[q], 16)
                wait_reuse(sp, u_full, N, Q)
                sp.dma_start(us[q][:, :], u_in[:, bass.ds(N, 1), :].rearrange("p n d -> p (n d)"))\
                  .then_inc(u_ld[q], 16)

            def step(b, n, N, q, one, two, three, turn, prepare, load):
                if load:
                    load_tile(N + Q, q)
                if one:
                    sp.wait_ge(x2_done, N + 1)
                    sp.dma_start(x2_out[:, bass.ds(N, 1), :].rearrange("p n d -> p (n d)"), x2[q][:, :])\
                      .then_inc(x2_st[q], 16)

            load_tile = load
            for b in range(B):
                for n in range(Q):
                    load_tile(b * NTB + n, n)
                if b == 0:
                    for tile, w in ((w2, W2), (wf, WQT), (wk, WK)):
                        sp.dma_start(tile[:, :, :, :].bitcast(F32), scr["w"][w]).then_inc(const_in, 16)
                    sp.dma_start(wv[:, :, :], scr["wv"]).then_inc(const_in, 16)
                over_steps(sp, b, step)
            for q in range(Q):
                sp.wait_ge(x2_st[q], 16 * B * NTB // Q)

        @block.gpsimd
        def _(pool):
            def prepare_tile(N, q):
                p = q % 2
                pool.wait_ge(prep, PREP * (N + 1))
                nc.gpsimd.tensor_tensor(xq[p][:, :], xq[p][:, :], magic[:, p, :], ALU.subtract).then_inc(q_sub, 1)
                wait_reuse(pool, x2_done, N, Q)
                nc.gpsimd.tensor_tensor(xb[q][:, :], xs[q][:, :], res_bias[:, :], ALU.add).then_inc(xb_done, 1)
                pool.wait_ge(q_sub, N + 1)
                nc.gpsimd.tensor_tensor(xq[p][:, :].rearrange("p (b e) -> p b e", e=QBLOCK),
                                        xq[p][:, :].rearrange("p (b e) -> p b e", e=QBLOCK),
                                        q_scale[:, p, :].unsqueeze(2).broadcast_to([P, NBL, QBLOCK]),
                                        ALU.mult).then_inc(q_done, 1)

            def step(b, n, N, q, one, two, three, turn, prepare, load):
                if one:
                    p = q % 2
                    pool.wait_ge(st3, N + 1)
                    nc.gpsimd.tensor_tensor(rstd[p][:, :], var_eps[:, :], keep["neg_half"][:, 0:1], ALU.pow)\
                      .then_inc(rstd_done, 1)
                    pool.wait_ge(rstd_done, N + 1)
                    nc.gpsimd.tensor_copy(keep["rstd1"][:, bass.ds(N, 1)], rstd[p][:, :])
                    nc.gpsimd.tensor_copy(keep["mean1"][:, bass.ds(N, 1)], moments[p][:, 0:1])
                if prepare:
                    prepare_tile(N + 2, (q + 2) % Q)
                if two:
                    pool.wait_ge(kr_done, N)
                    pool.wait_ge(kacc_done, N + b)
                    nc.gpsimd.tensor_tensor(kacc[:, :], kacc[:, :], kr[(q - 1) % 2][:, :], ALU.add)\
                      .then_inc(kacc_done, 1)

            nc.gpsimd.memset(ones[:, :], 1.0).then_inc(set_done, 1)
            nc.gpsimd.memset(zeros[:, :].bitcast(F32), 0.0).then_inc(set_done, 1)
            nc.gpsimd.memset(keep["kv"][:, :, :, :], 0.0).then_inc(set_done, 1)
            pool.wait_ge(const_in, 16 * 7)
            nc.gpsimd.tensor_tensor(res_bias[:, :], res_bias[:, :], ffn_bias[:, :], ALU.add).then_inc(bias_done, 1)
            pool.wait_ge(bias_done, 1)
            for b in range(B):
                if b:
                    pool.wait_ge(ks_full, b)
                nc.gpsimd.memset(kacc[:, :], 0.0).then_inc(kacc_done, 1)
                for n in range(2):
                    prepare_tile(b * NTB + n, n)
                over_steps(pool, b, step)

        @block.scalar
        def _(act):
            def step(b, n, N, q, one, two, three, turn, prepare, load):
                p = q % 2
                if two:
                    act.wait_ge(n_full, N)
                    nc.scalar.activation(nt[1 - p][:, 0, :, :], BA[:, :].rearrange("p (k t) -> p k t", k=KT),
                                         ACT.Copy).then_inc(n_hi, 1)
                if turn:
                    turned(N + 1, 1 - p)
                if one:
                    act.wait_ge(xn_done, N + 1)
                    nc.scalar.activation(nat[q][:, 0, :], xn[p][:, :], ACT.Copy).then_inc(nat_hi, 1)
                if two:
                    M = N - 1
                    act.wait_ge(kb_done, N)
                    if not (isinstance(M, int) and M < 2):
                        act.wait_ge(kacc_done, M - 1 + b)
                    nc.scalar.activation(kr[1 - p][:, :], kb[:, :], ACT.Relu).then_inc(kr_done, 1)
                    act.wait_ge(kr_done, N)
                    nc.scalar.activation(kh[1 - p][:, 0, :], kr[1 - p][:, :], ACT.Copy).then_inc(k_hi, 1)

            def turned(N, p):
                act.wait_ge(u_full, N + 1)
                nc.scalar.activation(ut[p][:, 0, :, :], BA[:, :].rearrange("p (k t) -> p k t", k=KT),
                                     ACT.Copy).then_inc(u_hi, 1)
                act.wait_ge(q_full, N + 1)
                nc.scalar.activation(qt[p][:, 0, :, :], BB[:, :].rearrange("p (k t) -> p k t", k=KT),
                                     ACT.Copy).then_inc(q_hi, 1)

            load_row(act, res_bias, ins["L0_attn_w2_b"]).then_inc(const_in, 16)
            load_row(act, ffn_bias, ins["L0_ffn_bias"]).then_inc(const_in, 16)
            load_row(act, bk, ins["L1_attn_bk"]).then_inc(const_in, 16)
            for b in range(B):
                turned(b * NTB, 0)
                over_steps(act, b, step)
                act.wait_ge(g_full, b + 1)
                for c in range(KT):
                    nc.scalar.activation(gt[:, c, :], BG[c][:, :], ACT.Copy).then_inc(g_done, 1)

        @block.vector
        def _(dve):
            def low(bank, tile, hi_sem, lo_sem, n):
                dve.wait_ge(hi_sem, n)
                nc.vector.tensor_tensor(tile[:, 1, :, :], bank[:, :].rearrange("p (k t) -> p k t", k=KT),
                                        tile[:, 0, :, :].bitcast(F32), ALU.subtract).then_inc(lo_sem, 1)

            def prepare_tile(N, q):
                p = q % 2
                k = [0]

                def link(ins_):
                    k[0] += 1
                    ins_.then_inc(prep, 1)
                    if k[0] < PREP:
                        dve.wait_ge(prep, PREP * N + k[0])

                blocks = xq[p][:, :].rearrange("p (b e) -> p b e", e=QBLOCK)
                dve.wait_ge(x_ld[q], (N - q) * (16 // Q) + 16)
                wait_reuse(dve, q_full, N, 2)
                link(nc.vector.tensor_scalar(xq[p][:, :], xs[q][:, :], keep["mean0"][:, bass.ds(N, 1)],
                                             keep["rstd0"][:, bass.ds(N, 1)], ALU.subtract, ALU.mult))
                link(nc.vector.tensor_reduce(q_max[:, :], blocks, AX.X, ALU.max, apply_absolute_value=True))
                link(nc.vector.tensor_scalar(q_scale[:, p, :], q_max[:, :], 1.0 / FP6_MAX, SCALE_EPS,
                                             ALU.mult, ALU.max))
                link(nc.vector.reciprocal(q_inv[:, :], q_scale[:, p, :]))
                link(nc.vector.tensor_tensor(blocks, blocks, q_inv[:, :].unsqueeze(2).broadcast_to([P, NBL, QBLOCK]),
                                             ALU.mult))
                link(nc.vector.tensor_scalar(magic[:, p, :].bitcast(U32), xq[p][:, :].bitcast(U32), EXPONENT_BITS,
                                             None, ALU.bitwise_and))
                link(nc.vector.tensor_scalar(magic[:, p, :], magic[:, p, :], 1.0, ROUND_MAGIC, ALU.max, ALU.mult))
                link(nc.vector.tensor_tensor(xq[p][:, :], xq[p][:, :], magic[:, p, :], ALU.add))

            def step(b, n, N, q, one, two, three, turn, prepare, load):
                p = q % 2
                if two:
                    low(BA, nt[1 - p], n_hi, n_lo, N)
                if one:
                    dve.wait_ge(x2_full, N + 1)
                    dve.wait_ge(xb_done, N + 1)
                    if not (isinstance(N, int) and N < Q):
                        dve.wait_ge(x2_st[q], (N - q) * (16 // Q))
                    nc.vector.tensor_tensor(x2[q][:, :], BX[:, :], xb[q][:, :], ALU.add).then_inc(x2_done, 1)
                    dve.wait_ge(x2_done, N + 1)
                    nc.vector.bn_stats(stats[:, :], x2[q][:, :]).then_inc(st1, 1)
                    dve.wait_ge(st1, N + 1)
                    nc.vector.memset(keep["beat"][:, :], 0.0)
                    nc.vector.bn_aggr(moments[p][:, :], stats[:, :]).then_inc(st2, 1)
                    dve.wait_ge(st2, N + 1)
                    nc.vector.tensor_scalar(var_eps[:, :], moments[p][:, 1:2], LN_EPS, None, ALU.add)\
                      .then_inc(st3, 1)
                if turn:
                    low(BA, ut[1 - p], u_hi, u_lo, N + 2)
                    low(BB, qt[1 - p], q_hi, q_lo, N + 2)
                if one:
                    dve.wait_ge(rstd_done, N + 1)
                    wait_reuse(dve, n_full, N, 2)
                    nc.vector.tensor_scalar(xn[p][:, :], x2[q][:, :], moments[p][:, 0:1], rstd[p][:, :],
                                            ALU.subtract, ALU.mult).then_inc(xn_done, 1)
                    dve.wait_ge(nat_hi, N + 1)
                    nc.vector.tensor_tensor(nat[q][:, 1, :], xn[p][:, :], nat[q][:, 0, :].bitcast(F32),
                                            ALU.subtract).then_inc(nat_lo, 1)
                if prepare:
                    prepare_tile(N + 2, (q + 2) % Q)
                if two:
                    dve.wait_ge(k_full, N)
                    wait_reuse(dve, kr_done, N - 1, 1)
                    nc.vector.tensor_tensor(kb[:, :], BK[:, :], bk[:, :], ALU.add).then_inc(kb_done, 1)
                    dve.wait_ge(k_hi, N)
                    nc.vector.tensor_tensor(kh[1 - p][:, 1, :], kr[1 - p][:, :], kh[1 - p][:, 0, :].bitcast(F32),
                                            ALU.subtract).then_inc(k_lo, 1)

            dve.wait_ge(const_in, 16 * 7)
            for b in range(B):
                for n in range(2):
                    prepare_tile(b * NTB + n, n)
                low(BA, ut[0], u_hi, u_lo, b * NTB + 1)
                low(BB, qt[0], q_hi, q_lo, b * NTB + 1)
                over_steps(dve, b, step)
                dve.wait_ge(ks_full, b + 1)
                nc.vector.tensor_copy(ksum_row[:, :], BA[0:1, :]).then_inc(ks_done, 1)
                dve.wait_ge(kv_full, b + 1)
                dve.wait_ge(set_done, 3)
                HD = D // HEADS
                for j in range(P // HD):
                    rows = slice(j * HD, (j + 1) * HD)
                    nc.vector.tensor_copy(keep["kv"][rows, b, :, j * HD:(j + 1) * HD],
                                          BX[rows, :].rearrange("p (t c) -> p t c", t=KT)[:, :, j * HD:(j + 1) * HD])
                    ins_ = nc.vector.tensor_copy(keep["kv"][rows, b, :, P + j:P + j + 1],
                                                 BB[rows, 0:KT].unsqueeze(2))
                ins_.then_inc(kv_done, 1)

        @block.tensor
        def _(pe):
            def turn_in(dst, src, s):
                for kt in range(KT):
                    mm = pe.transpose(dst[:, kt * P:(kt + 1) * P], src[:, kt * P:(kt + 1) * P], ident[:, :])
                mm.then_inc(s, 1)

            def turn_next(N, q, after):
                pe.wait_ge(u_ld[q], (N - q) * (16 // Q) + 16)
                if after:
                    pe.wait_ge(n_lo, N - 1)
                turn_in(BA, us[q], u_full)
                pe.wait_ge(q_done, N + 1)
                turn_in(BB, xq[q % 2], q_full)

            def parts(tile, kt):
                return [tile[:, j, kt, :] for j in range(2)]

            def step(b, n, N, q, one, two, three, turn, prepare, load):
                p = q % 2
                if one:
                    if not (isinstance(N, int) and N == 0):
                        pe.wait_ge(x2_done, N)
                    pe.wait_ge(u_lo, N + 1)
                    for kt in range(KT):
                        split_products(pe, BX[:, :], parts(ut[p], kt), parts(w2, kt), kt == 0, False)
                    pe.wait_ge(q_lo, N + 1)
                    for kt in range(KT):
                        mm = split_products(pe, BX[:, :], parts(qt[p], kt), parts(wf, kt), False, kt == KT - 1)
                    mm.then_inc(x2_full, 1)
                if two:
                    pe.wait_ge(xn_done, N)
                    turn_in(BA, xn[1 - p], n_full)
                if turn:
                    turn_next(N + 1, (q + 1) % Q, two)
                if three:
                    M = N - 2
                    pe.wait_ge(nat_lo, M + 1)
                    pe.wait_ge(k_lo, M + 1)
                    s, r = nat[(q - 2) % Q], kh[p]
                    for c in range(KT):
                        cols = slice(c * P, (c + 1) * P)
                        for i, j in ((0, 0), (0, 1), (1, 0)):
                            mm = pe.matmul(BG[c][:, :], s[:, i, cols], r[:, j, :], start=False, stop=False,
                                           skip_group_check=True)
                if two:
                    pe.wait_ge(n_lo, N)
                    wait_reuse(pe, kb_done, N - 1, 1)
                    for kt in range(KT):
                        mm = split_products(pe, BK[:, :], parts(nt[1 - p], kt), parts(wk, kt), kt == 0, kt == KT - 1)
                    mm.then_inc(k_full, 1)

            pe.wait_ge(set_done, 3)
            pe.wait_ge(const_in, 16 * 7)
            for b in range(B):
                if b:
                    pe.wait_ge(g_done, KT * b)
                    pe.wait_ge(kv_done, b)
                for c in range(KT):
                    pe.matmul(BG[c][:, :], zeros[:, 0:P], zeros[:, :], start=True, stop=False,
                              skip_group_check=True)
                turn_next(b * NTB, 0, False)
                over_steps(pe, b, step)
                pe.matmul(BG[0][:, :], zeros[:, 0:P], zeros[:, :], start=False, stop=True,
                          skip_group_check=True).then_inc(g_full, 1)
                pe.wait_ge(kacc_done, (b + 1) * NTB + b + 1)
                pe.matmul(BA[0:1, :], ones[:, :], kacc[:, :], start=True, stop=True)
                for t in range(KT):
                    mm = pe.matmul(BB[:, t:t + 1], kacc[:, t * P:(t + 1) * P], ones[:, :], start=True, stop=True)
                mm.then_inc(ks_full, 1)
                pe.wait_ge(g_done, KT * (b + 1))
                pe.wait_ge(ks_done, b + 1)
                for t in range(KT):
                    cols = slice(t * P, (t + 1) * P)
                    for c in range(KT):
                        pe.matmul(BX[:, cols], gt[:, c, cols], wv[:, c, cols], start=(c == 0), stop=False)
                    mm = pe.matmul(BX[:, cols], ksum_row[:, cols], keep["bv_row"][:, cols], start=False, stop=True)
                mm.then_inc(kv_full, 1)


def phase_second_layer(nc, sh, ins, scr, keep, banks):
    KT, D, GT, GN, NG, NGB, B = sh.KT, sh.D, sh.GT, sh.GN, sh.NG, sh.NGB, sh.B
    HD = D // HEADS
    HP = P // HD
    KVC = P + HP
    x2_in = scr["x2"].rearrange("(g t p) d -> p g t d", t=GT, p=P)
    out_d = scr["out"].rearrange("b s d -> (b s) d").rearrange("(g t p) d -> p g t d", t=GT, p=P)
    with ExitStack() as ctx:
        def sb(name, shape, dt=F32):
            return ctx.enter_context(nc.sbuf_tensor(name, shape, dt))

        def sem(name):
            return keep["semaphores"].enter_context(nc.semaphore(name))

        wk, wq, wr, wv = [sb(f"e_w{i}", [P, 2, KT, D], F32R) for i in range(4)]
        x2 = [sb(f"e_x2{i}", [P, GT, D]) for i in range(2)]
        xn = sb("e_xn", [P, GT, D])
        xt = sb("e_xt", [P, KT, GN + 1])
        ring = [sb(f"e_ring{i}", [P, 2, KT, GN], F32R) for i in range(2)]
        prev = [sb(f"e_prev{i}", [P, GN]) for i in range(2)]
        mixed = [sb(f"e_mixed{i}", [P, GN]) for i in range(2)]
        keys = sb("e_keys", [P, 2, KT, GN], F32R)
        kr = [sb(f"e_kr{i}", [P, GN]) for i in range(2)]
        kk = sb("e_kk", [P, GN])
        qt = sb("e_qt", [P, KT, GN])
        gate = sb("e_gate", [P, GT, D])
        ff = [sb(f"e_ff{i}", [P, D]) for i in range(2)]
        att = [sb(f"e_att{i}", [P, D]) for i in range(2)]
        y = [sb(f"e_y{i}", [P, D]) for i in range(GT)]
        den = sb("e_den", [P, 2, 2, HP])
        rden = sb("e_rden", [P, 2, 2, HP])
        stats = sb("e_stats", [P, 6])
        moments = [sb(f"e_moments{i}", [P, 2]) for i in range(2)]
        var_eps = sb("e_var_eps", [P, 1])
        rstd = [sb(f"e_rstd{i}", [P, 1]) for i in range(2)]
        gamma = sb("e_gamma", [P, D])
        beta = sb("e_beta", [P, D])
        rest_k = sb("e_rest_k", [P, KT])
        rest_r = sb("e_rest_r", [P, KT])

        const_in = sem("e_const_in")
        x_ld = [sem(f"e_x_ld{i}") for i in range(2)]
        o_st = [sem(f"e_o_st{i}") for i in range(2)]
        set_done = sem("e_set_done")
        xn_done = sem("e_xn_done")
        t_full, xt_done = sem("e_t_full"), sem("e_xt_done")
        halo = sem("e_halo")
        prev_done, mix_done = sem("e_prev_done"), sem("e_mix_done")
        hi_done, lo_done = sem("e_hi_done"), sem("e_lo_done")
        k_full, kr_done, kk_done, kh_done, kl_done = [sem(f"e_k{i}") for i in range(5)]
        q_full, q_done = sem("e_q_full"), sem("e_q_done")
        r_full, gate_done = sem("e_r_full"), sem("e_gate_done")
        v_full, ff_done = sem("e_v_full"), sem("e_ff_done")
        c_full, den_done, rden_done, c_done = [sem(f"e_c{i}") for i in range(4)]
        again_done, base_done, sum_done = sem("e_again_done"), sem("e_base_done"), sem("e_sum_done")
        st1, st2, st3 = sem("e_st1"), sem("e_st2"), sem("e_st3")
        rstd_done, norm_done, scaled = sem("e_rstd_done"), sem("e_norm_done"), sem("e_scaled")
        shifted, out_done = sem("e_shifted"), sem("e_out_done")

        TB, KQB, RVB, CB = banks[0:2], banks[2:4], banks[4:6], banks[6:8]
        ident = keep["ident"]
        block = ctx.enter_context(nc.Block("second_layer"))

        def over_groups(eng, body):
            for b in range(B):
                lo, hi = b * NGB // 2, (b + 1) * NGB // 2
                if b == 0:
                    body(0, 0, 0, True, False)
                    body(0, 1, 1, False, False)
                    lo += 1
                if b == B - 1:
                    hi -= 1
                if hi > lo:
                    with eng.Fori(lo, hi) as i:
                        body(b, i * 2, 0, False, False)
                        body(b, i * 2 + 1, 1, False, False)
                if b == B - 1:
                    body(b, NG - 2, 0, False, False)
                    body(b, NG - 1, 1, False, True)

        @block.sync
        def _(sp):
            def load(g, h):
                sp.dma_start(x2[h][:, :, :], x2_in[:, bass.ds(g, 1), :, :].rearrange("p g t d -> p (g t) d"))\
                  .then_inc(x_ld[h], 16)

            def body(b, g, h, first, last):
                sp.wait_ge(x_ld[h], slot_dmas(g, h) + 16)
                if not last:
                    if not first:
                        sp.wait_ge(o_st[1 - h], slot_dmas(g + 1, 1 - h))
                    load(g + 1, 1 - h)
                sp.wait_ge(out_done, GT * (g + 1))
                sp.wait_ge(xn_done, GT * (g + 1))
                sp.wait_ge(again_done, GT * (g + 1))
                sp.dma_start(out_d[:, bass.ds(g, 1), :, :].rearrange("p g t d -> p (g t) d"), x2[h][:, :, :])\
                  .then_inc(o_st[h], 16)

            load(0, 0)
            for tile, w in ((wk, WKF), (wq, WQ), (wr, WR), (wv, WVF)):
                sp.dma_start(tile[:, :, :, :].bitcast(F32), scr["w"][w]).then_inc(const_in, 16)
            over_groups(sp, body)
            for h in range(2):
                sp.wait_ge(o_st[h], 16 * NG // 2)

        @block.gpsimd
        def _(pool):
            def body(b, g, h, first, last):
                pool.wait_ge(x_ld[h], slot_dmas(g, h) + 16)
                if not (isinstance(g, int) and g < 2):
                    pool.wait_ge(o_st[h], slot_dmas(g, h))
                for t in range(GT + 2):
                    if t < GT:
                        n = g * GT + t
                        pool.wait_ge(ff_done, n + 1)
                        pool.wait_ge(again_done, n + 1)
                        nc.gpsimd.tensor_tensor(x2[h][:, t, :], x2[h][:, t, :], ff[t % 2][:, :], ALU.add)\
                          .then_inc(base_done, 1)
                        pool.wait_ge(c_done, 2 * (n + 1))
                        nc.gpsimd.tensor_tensor(y[t][:, :], y[t][:, :], att[t % 2][:, :], ALU.add)\
                          .then_inc(sum_done, 1)
                    if 1 <= t <= GT:
                        n = g * GT + t - 1
                        pool.wait_ge(st3, n + 1)
                        nc.gpsimd.tensor_tensor(rstd[(t - 1) % 2][:, :], var_eps[:, :], keep["neg_half"][:, 0:1],
                                                ALU.pow).then_inc(rstd_done, 1)
                    if t >= 2:
                        n = g * GT + t - 2
                        tile = y[t - 2]
                        pool.wait_ge(scaled, n + 1)
                        nc.gpsimd.tensor_tensor(tile[:, :], tile[:, :], beta[:, :], ALU.add).then_inc(shifted, 1)
                        pool.wait_ge(shifted, n + 1)
                        pool.wait_ge(base_done, n + 1)
                        nc.gpsimd.tensor_tensor(x2[h][:, t - 2, :], x2[h][:, t - 2, :], tile[:, :], ALU.add)\
                          .then_inc(out_done, 1)

            pool.wait_ge(const_in, 16 * 6)
            over_groups(pool, body)

        @block.scalar
        def _(act):
            def low_half(src, kt, slot, count):
                nc.scalar.activation(ring[slot][:, 0, kt, :], src, ACT.Copy).then_inc(hi_done, 1)

            def mix_set(g, slot, j, rest):
                m = j // 2
                for kt in range(KT + 1):
                    if kt < KT:
                        prev_term(g, m, kt, rest)
                    if kt:
                        mix_high(g, slot, m, kt - 1)

            def prev_term(g, m, kt, rest):
                n = g * 8 + (4 * m + kt)
                if m == 0:
                    act.wait_ge(xt_done, KT * g + kt + 1)
                    act.wait_ge(halo, g + 1)
                wait_reuse(act, mix_done, n, 2)
                nc.scalar.activation(prev[kt % 2][:, :], xt[:, kt, 0:GN], ACT.Copy, scale=rest[:, kt:kt + 1])\
                  .then_inc(prev_done, 1)

            def mix_high(g, slot, m, kt):
                act.wait_ge(mix_done, g * 8 + (4 * m + kt + 1))
                low_half(mixed[kt % 2][:, :], kt, slot, None)

            def turned(g, kt):
                act.wait_ge(t_full, KT * g + kt + 1)
                act.wait_ge(halo, g + 1)
                nc.scalar.activation(xt[:, kt, 1:GN + 1], TB[kt % 2][:, :], ACT.Copy).then_inc(xt_done, 1)

            def body(b, g, h, first, last):
                for m in range(KT):
                    act.wait_ge(k_full, KT * g + m + 1)
                    wait_reuse(act, kk_done, g * KT + m, 2)
                    nc.scalar.activation(kr[m % 2][:, :], KQB[m % 2][:, :], ACT.Relu).then_inc(kr_done, 1)
                    act.wait_ge(kr_done, KT * g + m + 1)
                    nc.scalar.activation(keys[:, 0, m, :], kr[m % 2][:, :], ACT.Square).then_inc(kh_done, 1)
                for m in range(KT):
                    prev_term(g, 1, m, rest_r)
                    act.wait_ge(q_full, KT * g + m + 1)
                    if not (isinstance(g, int) and g == 0):
                        act.wait_ge(c_full, GT * g)
                    nc.scalar.activation(qt[:, m, :], KQB[m % 2][:, :], ACT.Relu,
                                         bias=keep["bq_col"][:, m:m + 1]).then_inc(q_done, 1)
                    mix_high(g, h, 1, m)
                for t in range(GT):
                    if not last:
                        turned(g + 1, t)
                        prev_term(g + 1, 0, t, rest_k)
                    act.wait_ge(r_full, GT * g + t + 1)
                    if not (isinstance(g, int) and g == 0):
                        act.wait_ge(ff_done, GT * g)
                    nc.scalar.activation(gate[:, t, :], RVB[t % 2][:, :], ACT.Sigmoid).then_inc(gate_done, 1)
                    if not last:
                        mix_high(g + 1, 1 - h, 0, t)
                if not last:
                    act.wait_ge(r_full, GT * (g + 1))
                    for kt in range(KT):
                        act.wait_ge(xt_done, KT * (g + 1) + kt + 1)
                        low_half(xt[:, kt, 1:GN + 1], kt, h, None)

            load_row(act, gamma, ins["L1_attn_gamma"]).then_inc(const_in, 16)
            load_row(act, beta, ins["L1_attn_beta"]).then_inc(const_in, 16)
            act.wait_ge(set_done, 2)
            for kt in range(KT):
                turned(0, kt)
                prev_term(0, 0, kt, rest_k)
                mix_high(0, 0, 0, kt)
            for kt in range(KT):
                act.wait_ge(xt_done, kt + 1)
                low_half(xt[:, kt, 1:GN + 1], kt, 1, None)
            over_groups(act, body)

        @block.vector
        def _(dve):
            def normalise(g, h):
                dve.wait_ge(x_ld[h], slot_dmas(g, h) + 16)
                if not (isinstance(g, int) and g == 0):
                    dve.wait_ge(t_full, KT * g)
                for t in range(GT):
                    n = g * GT + t
                    nc.vector.tensor_scalar(xn[:, t, :], x2[h][:, t, :], keep["mean1"][:, bass.ds(n, 1)],
                                            keep["rstd1"][:, bass.ds(n, 1)], ALU.subtract, ALU.mult)\
                      .then_inc(xn_done, 1)

            def carry_over(g):
                nc.vector.tensor_scalar(xt[:, :, 0:1], xt[:, :, GN:GN + 1], keep["batch_mask"][:, bass.ds(g, 1)],
                                        None, ALU.mult).then_inc(halo, 1)

            def mix(g, slot, m, kt, mu):
                dve.wait_ge(prev_done, g * 8 + (4 * m + kt + 1))
                wait_reuse(dve, hi_done, g * 12 + (8 * m + kt), 2)
                nc.vector.scalar_tensor_tensor(mixed[kt % 2][:, :], xt[:, kt, 1:GN + 1], mu[:, kt:kt + 1],
                                               prev[kt % 2][:, :], ALU.mult, ALU.add).then_inc(mix_done, 1)
                dve.wait_ge(hi_done, g * 12 + (8 * m + kt + 1))
                rest(slot, kt, mixed[kt % 2][:, :])

            def rest(slot, kt, src):
                nc.vector.tensor_tensor(ring[slot][:, 1, kt, :], src, ring[slot][:, 0, kt, :].bitcast(F32),
                                        ALU.subtract).then_inc(lo_done, 1)

            def plain(g, slot, kt):
                dve.wait_ge(hi_done, g * 12 + (4 + kt + 1))
                rest(slot, kt, xt[:, kt, 1:GN + 1])

            def body(b, g, h, first, last):
                for m in range(KT):
                    dve.wait_ge(kr_done, KT * g + m + 1)
                    wait_reuse(dve, kl_done, g * KT + m, 1)
                    nc.vector.tensor_tensor(kk[:, :], kr[m % 2][:, :], kr[m % 2][:, :], ALU.mult).then_inc(kk_done, 1)
                    dve.wait_ge(kk_done, KT * g + m + 1)
                    dve.wait_ge(kh_done, KT * g + m + 1)
                    nc.vector.tensor_tensor(keys[:, 1, m, :], kk[:, :], keys[:, 0, m, :].bitcast(F32), ALU.subtract)\
                      .then_inc(kl_done, 1)
                if not last:
                    normalise(g + 1, 1 - h)
                for kt in range(KT):
                    mix(g, h, 1, kt, keep["mu_r_col"])
                if not last:
                    carry_over(g + 1)
                    for t in range(GT):
                        mix(g + 1, 1 - h, 0, t, keep["mu_k_col"])
                for t in range(GT + 2):
                    if t < GT:
                        tile_products(g, h, t)
                    if not last and t < GT:
                        plain(g + 1, h, t)
                    if 1 <= t <= GT:
                        tile_stats(g, t - 1)
                    if t >= 2:
                        tile_norm(g, t - 2)

            def tile_products(g, h, t):
                n = g * GT + t
                wait_reuse(dve, out_done, n, GT)
                nc.vector.tensor_scalar(y[t][:, :], x2[h][:, t, :], keep["mean1"][:, bass.ds(n, 1)],
                                        keep["rstd1"][:, bass.ds(n, 1)], ALU.subtract, ALU.mult)\
                  .then_inc(again_done, 1)
                dve.wait_ge(v_full, n + 1)
                dve.wait_ge(gate_done, n + 1)
                wait_reuse(dve, base_done, n, 2)
                nc.vector.tensor_tensor(ff[t % 2][:, :], RVB[t % 2][:, :], gate[:, t, :], ALU.mult)\
                  .then_inc(ff_done, 1)
                dve.wait_ge(c_full, n + 1)
                for c in range(2):
                    sums = CB[c][:, 0:2 * KVC].rearrange("p (a x) -> p a x", a=2)
                    nc.vector.tensor_scalar(den[:, c, :, :], sums[:, :, P:KVC], DENOM_EPS, None, ALU.max)\
                      .then_inc(den_done, 1)
                dve.wait_ge(den_done, 2 * (n + 1))
                nc.vector.reciprocal(rden[:, :, :, :].rearrange("p c a j -> p (c a j)"),
                                     den[:, :, :, :].rearrange("p c a j -> p (c a j)")).then_inc(rden_done, 1)
                dve.wait_ge(rden_done, n + 1)
                wait_reuse(dve, sum_done, n, 2)
                for c in range(2):
                    sums = CB[c][:, 0:2 * KVC].rearrange("p (a x) -> p a x", a=2)[:, :, 0:P]
                    nc.vector.tensor_tensor(
                        att[t % 2][:, c * 2 * P:(c + 1) * 2 * P].rearrange("p (a j d) -> p a j d", a=2, j=HP),
                        sums.rearrange("p a (j d) -> p a j d", j=HP),
                        rden[:, c, :, :].unsqueeze(3).broadcast_to([P, 2, HP, HD]), ALU.mult).then_inc(c_done, 1)

            def tile_stats(g, t):
                n = g * GT + t
                dve.wait_ge(sum_done, n + 1)
                nc.vector.bn_stats(stats[:, :], y[t][:, :]).then_inc(st1, 1)
                dve.wait_ge(st1, n + 1)
                nc.vector.memset(keep["beat"][:, :], 0.0)
                nc.vector.bn_aggr(moments[t % 2][:, :], stats[:, :]).then_inc(st2, 1)
                dve.wait_ge(st2, n + 1)
                wait_reuse(dve, rstd_done, n, 1)
                nc.vector.tensor_scalar(var_eps[:, :], moments[t % 2][:, 1:2], LN_EPS, None, ALU.add).then_inc(st3, 1)

            def tile_norm(g, t):
                n = g * GT + t
                dve.wait_ge(rstd_done, n + 1)
                nc.vector.tensor_scalar(y[t][:, :], y[t][:, :], moments[t % 2][:, 0:1], rstd[t % 2][:, :],
                                        ALU.subtract, ALU.mult).then_inc(norm_done, 1)
                dve.wait_ge(norm_done, n + 1)
                nc.vector.tensor_tensor(y[t][:, :], y[t][:, :], gamma[:, :], ALU.mult).then_inc(scaled, 1)

            for tile, mu in ((rest_k, keep["mu_k_col"]), (rest_r, keep["mu_r_col"])):
                nc.vector.tensor_scalar(tile[:, :], mu, -1.0, 1.0, ALU.mult, ALU.add).then_inc(set_done, 1)
            nc.vector.memset(xt[:, :, 0:1], 0.0).then_inc(halo, 1)
            normalise(0, 0)
            dve.wait_ge(const_in, 16 * 6)
            for kt in range(KT):
                mix(0, 0, 0, kt, keep["mu_k_col"])
            for kt in range(KT):
                plain(0, 1, kt)
            over_groups(dve, body)

        @block.tensor
        def _(pe):
            def turn(g, kt):
                if kt == 0:
                    pe.wait_ge(xn_done, GT * (g + 1))
                wait_reuse(pe, xt_done, g * KT + kt, 2)
                for t in range(GT):
                    mm = pe.transpose(TB[kt % 2][:, t * P:(t + 1) * P], xn[:, t, kt * P:(kt + 1) * P], ident[:, :])
                mm.then_inc(t_full, 1)

            def channels_out(g, j, slot, w, done):
                for m in range(KT):
                    if m >= 2:
                        pe.wait_ge(kr_done if j == 0 else q_done, KT * g + m - 1)
                    elif j == 1:
                        pe.wait_ge(kr_done, KT * g + m + 3)
                    elif not (isinstance(g, int) and g == 0):
                        pe.wait_ge(q_done, KT * g + m - 1)
                    for kt in range(KT):
                        if m == 0:
                            pe.wait_ge(lo_done, 12 * g + (4 * j + kt + 1))
                        mm = split_products(pe, KQB[m % 2][:, :],
                                            [w[:, i, kt, m * P:(m + 1) * P] for i in range(2)],
                                            [ring[slot][:, i, kt, :] for i in range(2)], kt == 0, kt == KT - 1)
                    mm.then_inc(done, 1)

            def tokens_out(t, left, w):
                for kt in range(KT):
                    mm = split_products(pe, RVB[t % 2][:, :],
                                        [left[:, i, kt, t * P:(t + 1) * P] for i in range(2)],
                                        [w[:, i, kt, :] for i in range(2)], kt == 0, kt == KT - 1)
                return mm

            def body(b, g, h, first, last):
                channels_out(g, 0, h, wk, k_full)
                channels_out(g, 1, 1 - h, wq, q_full)
                for t in range(GT):
                    if t == 0:
                        pe.wait_ge(lo_done, 12 * g + 12)
                    if t < 2:
                        if not first:
                            pe.wait_ge(ff_done, GT * g - 1 + t)
                    else:
                        pe.wait_ge(gate_done, GT * g + t - 1)
                    tokens_out(t, ring[h], wr).then_inc(r_full, 1)
                    if not last:
                        turn(g + 1, t)
                for t in range(GT):
                    n = g * GT + t
                    if t < 2:
                        pe.wait_ge(gate_done, n + 3)
                    else:
                        pe.wait_ge(ff_done, n - 1)
                    if t == 0:
                        pe.wait_ge(kl_done, KT * (g + 1))
                    tokens_out(t, keys, wv).then_inc(v_full, 1)
                    if not (first and t == 0):
                        pe.wait_ge(c_done, 2 * n)
                    for a in range(KT):
                        mm = pe.matmul(CB[a // 2][:, a % 2 * KVC:(a % 2 + 1) * KVC], qt[:, a, t * P:(t + 1) * P],
                                       keep["kv"][:, b, a, :], start=True, stop=True)
                    mm.then_inc(c_full, 1)

            for kt in range(KT):
                turn(0, kt)
            pe.wait_ge(const_in, 16 * 6)
            over_groups(pe, body)


INPUTS = ["L0_attn_x", "L0_attn_w1_w", "L0_attn_w1_b", "L0_attn_v1_w", "L0_attn_v1_b", "L0_attn_w2_w",
          "L0_attn_w2_b", "L0_attn_conv_w", "L0_attn_A", "L0_attn_B_ssm", "L0_attn_C_ssm", "L0_attn_D_ssm",
          "L0_ffn_weight", "L0_ffn_bias", "L1_attn_Wq", "L1_attn_bq", "L1_attn_Wk", "L1_attn_bk",
          "L1_attn_Wv", "L1_attn_bv", "L1_attn_gamma", "L1_attn_beta", "L1_ffn_W_r", "L1_ffn_W_k",
          "L1_ffn_W_v", "L1_ffn_mu_r", "L1_ffn_mu_k"]


def two_layer_kernel(nc, ins, out):
    sh = Shapes(ins["L0_attn_x"])
    KT, D, T, NT = sh.KT, sh.D, sh.T, sh.NT
    NS = ins["L0_attn_A"].shape[1]
    OCT = D // 8

    def dram(name, shape, dt=F32):
        return nc.dram_tensor(name, shape, dt, kind="Internal").ap()

    scr = {
        "w": dram("scr_w", [SPLIT_WEIGHTS, P, 2, KT, D]),
        "wv": dram("scr_wv", [P, KT, D]),
        "kern": dram("scr_kern", [D, 2 * P]),
        "state_in": dram("scr_state_in", [OCT, P, P]),
        "state_out": dram("scr_state_out", [D, NS, P]),
        "decay": dram("scr_decay", [D, NS]),
        "z": dram("scr_z", [T, D]),
        "v": dram("scr_v", [T, D]),
        "u": dram("scr_u", [T, D]),
        "x2": dram("scr_x2", [T, D]),
    }
    scr["state_out_rows"] = scr["state_out"].rearrange("(o c) s m -> o (c s) m", c=8)
    with ExitStack() as ctx:
        def sb(name, shape, dt=F32):
            return ctx.enter_context(nc.sbuf_tensor(name, shape, dt))

        keep = {
            "semaphores": ctx,
            "ident": sb("ident", [P, P]),
            "own_mask": sb("own_mask", [P, 8, NT]),
            "carry_mask": sb("carry_mask", [P, 8, NT]),
            "batch_mask": sb("batch_mask", [P, sh.NG]),
            "beat": sb("beat", [P, 1]),
            "neg_half": sb("neg_half", [P, 8]),
            "decay_col": sb("decay_col", [P, OCT]),
            "cols": sb("cols", [P, len(VECTORS) * KT]),
            "conv_col": sb("conv_col", [P, KT, 3]),
            "bv_row": sb("bv_row", [1, D]),
            "mean0": sb("mean0", [P, NT]),
            "rstd0": sb("rstd0", [P, NT]),
            "mean1": sb("mean1", [P, NT]),
            "rstd1": sb("rstd1", [P, NT]),
            "kv": sb("kv", [P, sh.B, KT, P + 4]),
        }
        for i, name in enumerate(["b1_col", "bq_col", "mu_r_col", "mu_k_col"]):
            keep[name] = keep["cols"][:, i * KT:(i + 1) * KT]
        banks = [ctx.enter_context(nc.psum_tensor(f"bank{i}", [P, 512], F32)) for i in range(8)]
        phases = [phase_tables, phase_project, phase_state_space, phase_mix, phase_second_layer]
        for phase in phases[:PHASES]:
            phase(nc, sh, ins, dict(scr, out=out), keep, banks)


PHASES = 5


def kernel(**inputs):
    import numpy as np
    import concourse.bacc as bacc
    from concourse.bass_utils import run_bass_kernel_spmd

    nc = bacc.Bacc("TRN2", target_bir_lowering=False, num_devices=1)
    arrays, ins = {}, {}
    for name in INPUTS:
        a = np.ascontiguousarray(inputs[name])
        arrays[f"in_{name}"] = a
        ins[name] = nc.dram_tensor(f"in_{name}", a.shape, mybir.dt.from_np(a.dtype), kind="ExternalInput").ap()
    out = nc.dram_tensor("out", inputs["L0_attn_x"].shape, F32, kind="ExternalOutput").ap()
    two_layer_kernel(nc, ins, out)
    r = run_bass_kernel_spmd(nc, [arrays], core_ids=[0])
    return r.results[0]["out"]
```

```python
from contextlib import ExitStack

import concourse.bass as bass
from concourse import mybir

P = 128
F32 = mybir.dt.float32
F32R = mybir.dt.float32r
U32 = mybir.dt.uint32
ALU = mybir.AluOpType
ACT = mybir.ActivationFunctionType
AX = mybir.AxisListType

LN_EPS = 1e-5
QBLOCK = 32
FP6_MAX = 7.5
SCALE_EPS = 1e-30
EXPONENT_BITS = 0x7F800000
ROUND_MAGIC = 1.5 * 2.0 ** 20
HEADS = 16
DENOM_EPS = 1e-6

WEIGHTS = ["L0_attn_w1_w", "L0_attn_v1_w", "L0_ffn_weight",
           "L0_attn_w2_w", "L1_attn_Wk", "L1_attn_Wv",
           "L1_ffn_W_k", "L1_attn_Wq", "L1_ffn_W_r", "L1_ffn_W_v"]

VECTORS = ["L0_attn_w1_b", "L1_attn_bq", "L1_ffn_mu_r", "L1_ffn_mu_k", "L0_attn_D_ssm"]


class Shapes:

    def __init__(self, x):
        self.B, self.S, self.D = x.shape
        self.KT = self.D // P
        self.T = self.B * self.S
        self.NT = self.T // P
        self.GT = 4
        self.GN = self.GT * P
        self.NG = self.T // self.GN
        self.NGB = self.NG // self.B
        self.NTB = self.NT // self.B
        assert self.D == 512 and self.NGB % 2 == 0 and self.T % self.GN == 0


def slot_dmas(g, h):
    return (g - h) * 8


def load_row(eng, tile, vector):
    return eng.dma_start(tile[:, :], vector.rearrange("(o d) -> o d", o=1).broadcast_to(list(tile.shape)))


def wait_reuse(eng, sem, n, lag, per=1):
    if not (isinstance(n, int) and n < lag):
        eng.wait_ge(sem, (n - (lag - 1)) * per)


def split_products(eng, out, lhs, rhs, first, last):
    hi, lo = 0, 1
    eng.matmul(out, lhs[hi], rhs[hi], start=first, stop=False)
    eng.matmul(out, lhs[hi], rhs[lo], start=False, stop=False)
    return eng.matmul(out, lhs[lo], rhs[hi], start=False, stop=last)


class WeightTurner:

    def __init__(self, nc, ins, sems, first, tiles, stages, banks, ident):
        self.nc, self.ins, self.sems, self.ident = nc, ins, sems, ident
        self.numbers = range(first, first + len(tiles))
        self.tiles = dict(zip(self.numbers, tiles))
        self.stages = {n: stages[(n - first) % len(stages)] for n in self.numbers}
        self.reused = {n for n in self.numbers if n - first >= len(stages)}
        self.lag = len(stages)
        self.banks, self.KT = banks, len(banks)

    def load(self, eng, some=None):
        for n in some or self.numbers:
            if n in self.reused:
                eng.wait_ge(self.sems["turned"], self.KT * (n - self.lag + 1))
            eng.dma_start(self.stages[n][:, :, :], self.ins[WEIGHTS[n]].rearrange("(t p) k -> p t k", p=P))\
               .then_inc(self.sems["in"][n % 3], 16)

    def wait_loaded(self, eng, n):
        eng.wait_ge(self.sems["in"][n % 3], 16 * (n // 3 + 1))

    def turn(self, pe, some=None):
        for n in some or self.numbers:
            self.wait_loaded(pe, n)
            for kt in range(self.KT):
                if n != self.numbers[0]:
                    pe.wait_ge(self.sems["rest"], self.KT * (n - 1) + kt + 1)
                for ot in range(self.KT):
                    mm = pe.transpose(self.banks[kt][:, ot * P:(ot + 1) * P],
                                      self.stages[n][:, ot, kt * P:(kt + 1) * P], self.ident[:, :])
                mm.then_inc(self.sems["turned"], 1)

    def round(self, act, some=None):
        for n in some or self.numbers:
            tile = self.tiles[n]
            for kt in range(self.KT):
                act.wait_ge(self.sems["turned"], self.KT * n + kt + 1)
                if len(tile.shape) == 4:
                    ins_ = self.nc.scalar.activation(tile[:, 0, kt, :], self.banks[kt][:, :], ACT.Copy)
                else:
                    half = tile.shape[2] // 2
                    ins_ = self.nc.scalar.activation(tile[:, kt, 0:half], self.banks[kt][:, 0:half], ACT.Copy)
                ins_.then_inc(self.sems["rounded"], 1)

    def rest(self, dve, some=None):
        for n in some or self.numbers:
            tile = self.tiles[n]
            for kt in range(self.KT):
                dve.wait_ge(self.sems["rounded"], self.KT * n + kt + 1)
                if len(tile.shape) == 4:
                    ins_ = self.nc.vector.tensor_tensor(tile[:, 1, kt, :], self.banks[kt][:, :],
                                                        tile[:, 0, kt, :].bitcast(F32), ALU.subtract)
                else:
                    half = tile.shape[2] // 2
                    ins_ = self.nc.vector.tensor_copy(tile[:, kt, half:], self.banks[kt][:, half:])
                ins_.then_inc(self.sems["rest"], 1)

    def wait_all(self, eng):
        eng.wait_ge(self.sems["rest"], self.KT * (self.numbers[-1] + 1))


def phase_tables(nc, sh, ins, scr, keep, banks):
    KT, D = sh.KT, sh.D
    NS = ins["L0_attn_A"].shape[1]
    GS = KT * NS
    with ExitStack() as ctx:
        def sb(name, shape, dt=F32):
            return ctx.enter_context(nc.sbuf_tensor(name, shape, dt))

        def sem(name):
            return keep["semaphores"].enter_context(nc.semaphore(name))

        w_nat = [sb(f"w_nat{i}", [P, KT, D]) for i in range(3)]
        wf = sb("a_wf", [P, 2, KT, D], F32R)
        q_work = sb("q_work", [P, KT * D])
        q_work2 = sb("q_work2", [P, KT * D])
        q_max = sb("q_max", [P, KT * D // QBLOCK])
        q_scale = sb("q_scale", [P, KT * D // QBLOCK])
        q_inv = sb("q_inv", [P, KT * D // QBLOCK])
        a_in = sb("a_in", [P, KT, NS])
        b_in = sb("b_in", [P, KT, NS])
        c_in = sb("c_in", [P, KT, NS])
        vec_rows = sb("vec_rows", [len(VECTORS) * KT, P])
        cb = sb("cb", [P, KT, NS])
        cb_sum = sb("cb_sum", [P, KT])
        a_exp = sb("a_exp", [P, GS])
        a_den = sb("a_den", [P, GS])
        a_pow = sb("a_pow", [P, 8, GS])
        out_rows = sb("out_rows", [P, GS, P])
        state_cols = sb("state_cols", [P, GS, P])
        kern = sb("kern", [P, KT, 2 * P])
        state_t = sb("state_t", [P, KT, P, NS])
        decay_rows = sb("decay_rows", [D // 8, P])

        ident_set = sem("a_ident_set")
        mask_set = sem("a_mask_set")
        q_step = sem("a_q_step")
        wf_out = sem("a_wf_out")
        small_in = sem("a_small_in")
        vec_in, vec_t, vec_done = sem("a_vec_in"), sem("a_vec_t"), sem("a_vec_done")
        a_exp_done = sem("a_exp_done")
        a_step = sem("a_step")
        r_step = sem("a_r_step")
        st_done = sem("a_st_done")
        dec_stored = sem("a_dec_stored")
        dec_in = sem("a_dec_in")
        dec_t = sem("a_dec_t")
        dec_done = sem("a_dec_done")
        tab_stored = sem("a_tab_stored")

        ident = keep["ident"]
        TB = banks[0:4]
        SBK = banks[4:6]
        DB = banks[6]
        STEPS = P.bit_length() - 1
        ROW_STEPS = 2 * STEPS + 5
        TABLE_STEPS = ROW_STEPS + 3
        NSB = GS // 4
        dec_d = scr["decay"]

        def quantise_weight(dve, w):
            turner.wait_loaded(dve, 2)
            flat = w[:, :, :].rearrange("p t k -> p (t k)")
            blocks = flat.rearrange("p (b e) -> p b e", e=QBLOCK)
            NB = q_max.shape[1]
            work = q_work[:, :].rearrange("p (b e) -> p b e", e=QBLOCK)
            nc.vector.tensor_reduce(q_max[:, :], blocks, AX.X, ALU.max, apply_absolute_value=True).then_inc(q_step, 1)
            dve.wait_ge(q_step, 1)
            nc.vector.tensor_scalar(q_scale[:, :], q_max[:, :], 1.0 / FP6_MAX, SCALE_EPS, ALU.mult, ALU.max)\
              .then_inc(q_step, 1)
            dve.wait_ge(q_step, 2)
            nc.vector.reciprocal(q_inv[:, :], q_scale[:, :]).then_inc(q_step, 1)
            dve.wait_ge(q_step, 3)
            nc.vector.tensor_tensor(work, blocks, q_inv[:, :].unsqueeze(2).broadcast_to([P, NB, QBLOCK]), ALU.mult)\
              .then_inc(q_step, 1)
            dve.wait_ge(q_step, 4)
            nc.vector.tensor_scalar(q_work2[:, :].bitcast(U32), q_work[:, :].bitcast(U32), EXPONENT_BITS, None,
                                    ALU.bitwise_and).then_inc(q_step, 1)
            dve.wait_ge(q_step, 5)
            nc.vector.tensor_scalar(q_work2[:, :], q_work2[:, :], 1.0, ROUND_MAGIC, ALU.max, ALU.mult)\
              .then_inc(q_step, 1)
            dve.wait_ge(q_step, 6)
            nc.vector.tensor_tensor(q_work[:, :], q_work[:, :], q_work2[:, :], ALU.add).then_inc(q_step, 1)
            dve.wait_ge(q_step, 7)
            nc.vector.tensor_tensor(q_work[:, :], q_work[:, :], q_work2[:, :], ALU.subtract).then_inc(q_step, 1)
            dve.wait_ge(q_step, 8)
            nc.vector.tensor_tensor(blocks, work, q_scale[:, :].unsqueeze(2).broadcast_to([P, NB, QBLOCK]), ALU.mult)\
              .then_inc(q_step, 1)

        turner = WeightTurner(nc, ins, keep["weight_sems"], 0, [keep["w1"], keep["v1"], wf], w_nat, TB, ident)
        block = ctx.enter_context(nc.Block("tables"))

        @block.sync
        def _(sp):
            turner.load(sp)
            turner.wait_all(sp)
            sp.dma_start(scr["wf"], wf[:, :, :, :].bitcast(F32)).then_inc(wf_out, 16)
            sp.wait_ge(wf_out, 16)

        @block.gpsimd
        def _(pool):
            nc.gpsimd.memset(ident[:, :], 0.0).then_inc(ident_set, 1)
            pool.wait_ge(ident_set, 1)
            nc.gpsimd.affine_select(out=ident[:, :], in_=ident[:, :], compare_op=ALU.not_equal, fill=1.0,
                                    base=0, pattern=[[-1, P]], channel_multiplier=1).then_inc(ident_set, 1)
            own, carry = keep["own_mask"], keep["carry_mask"]
            NCB = own.shape[2] // sh.B
            nc.gpsimd.memset(own[:, :, :], 1.0).then_inc(mask_set, 1)
            pool.wait_ge(mask_set, 1)
            nc.gpsimd.affine_select(out=own[:, :, :], in_=own[:, :, :], compare_op=ALU.is_ge, fill=0.0, base=0,
                                    pattern=[[-NS, 8], [0, own.shape[2]]], channel_multiplier=1).then_inc(mask_set, 1)
            pool.wait_ge(mask_set, 2)
            nc.gpsimd.affine_select(out=own[:, :, :], in_=own[:, :, :], compare_op=ALU.is_ge, fill=0.0, base=NS - 1,
                                    pattern=[[NS, 8], [0, own.shape[2]]], channel_multiplier=-1).then_inc(mask_set, 1)
            pool.wait_ge(mask_set, 3)
            for b in range(sh.B):
                nc.gpsimd.memset(own[:, :, (b + 1) * NCB - 1:(b + 1) * NCB], 0.0).then_inc(mask_set, 1)
            nc.gpsimd.memset(carry[:, :, :], 1.0).then_inc(mask_set, 1)
            pool.wait_ge(mask_set, 3 + sh.B + 1)
            for b in range(sh.B):
                nc.gpsimd.memset(carry[:, :, b * NCB:b * NCB + 1], 0.0).then_inc(mask_set, 1)
            nc.gpsimd.memset(keep["batch_mask"][:, :], 1.0).then_inc(mask_set, 1)
            pool.wait_ge(mask_set, 3 + 2 * sh.B + 2)
            for b in range(sh.B):
                nc.gpsimd.memset(keep["batch_mask"][:, b * sh.NGB:b * sh.NGB + 1], 0.0).then_inc(mask_set, 1)
            nc.gpsimd.memset(keep["neg_half"][:, :], -0.5).then_inc(mask_set, 1)

            nc.gpsimd.memset(state_cols[:, :, 0:1], 1.0).then_inc(r_step, 1)
            for j in range(STEPS):
                L = 1 << j
                pool.wait_ge(r_step, j + 1)
                pool.wait_ge(a_step, 2 + j)
                nc.gpsimd.tensor_tensor(state_cols[:, :, L:2 * L], state_cols[:, :, 0:L],
                                        a_pow[:, j, :].unsqueeze(2).broadcast_to([P, GS, L]),
                                        ALU.mult).then_inc(r_step, 1)

        @block.scalar
        def _(act):
            for name, tile in (("L0_attn_A", a_in), ("L0_attn_B_ssm", b_in), ("L0_attn_C_ssm", c_in)):
                act.dma_start(tile[:, :, :], ins[name].rearrange("(t p) s -> p t s", p=P)).then_inc(small_in, 16)
            for i, name in enumerate(VECTORS):
                act.dma_start(vec_rows[i * KT:(i + 1) * KT, :],
                              ins[name].rearrange("(t p) -> t p", p=P)).then_inc(vec_in, 16)
            act.dma_start(keep["conv_col"][:, :, :],
                          ins["L0_attn_conv_w"].rearrange("(t p) o k -> p t (o k)", p=P)).then_inc(small_in, 16)
            act.dma_start(keep["bv_row"][:, :], ins["L1_attn_bv"].rearrange("(o d) -> o d", o=1)).then_inc(small_in, 16)
            act.wait_ge(small_in, 16 * 5)
            act.activation(a_exp[:, :], a_in[:, :, :].rearrange("p t s -> p (t s)"), ACT.Exp,
                           scale=-1.0).then_inc(a_exp_done, 1)
            act.wait_ge(vec_t, 1)
            nc.scalar.activation(keep["cols"][:, :], DB[:, 0:len(VECTORS) * KT], ACT.Copy).then_inc(vec_done, 1)
            act.wait_ge(a_step, STEPS + 2)
            act.dma_start(dec_d.rearrange("(t p) s -> p t s", p=P),
                          a_pow[:, STEPS, :].rearrange("p (t s) -> p t s", t=KT)).then_inc(dec_stored, 16)
            turner.round(act, [0, 1])
            act.wait_ge(dec_stored, 16)
            act.dma_start(decay_rows[:, :], dec_d.rearrange("(o c) s -> o (c s)", c=8)).then_inc(dec_in, 16)
            act.wait_ge(dec_t, 1)
            act.activation(keep["decay_col"][:, :], DB[:, 0:D // 8], ACT.Copy).then_inc(dec_done, 1)
            act.wait_ge(a_step, ROW_STEPS)
            act.dma_start(scr["state_out"].rearrange("(t p) s m -> p t s m", p=P),
                          out_rows[:, :, :].rearrange("p (t s) m -> p t s m", t=KT)).then_inc(tab_stored, 16)
            for q in range(NSB):
                act.wait_ge(st_done, q + 1)
                act.activation(state_t[:, q * 4 // NS, :, q * 4 % NS:q * 4 % NS + 4].rearrange("p c s -> p s c"),
                               SBK[q % 2][:, :].rearrange("p (s c) -> p s c", s=4), ACT.Copy).then_inc(dec_done, 1)
            act.wait_ge(dec_done, NSB + 1)
            act.dma_start(scr["state_in"].rearrange("o k x -> k o x"),
                          state_t[:, :, :, :].rearrange("p t c s -> p (t c s)").rearrange("p (o x) -> p o x", x=P)
                          ).then_inc(tab_stored, 16)
            act.wait_ge(a_step, TABLE_STEPS)
            act.dma_start(scr["kern"].rearrange("(t p) j -> p t j", p=P), kern[:, :, :]).then_inc(tab_stored, 16)
            turner.round(act, [2])
            act.wait_ge(tab_stored, 48)

        @block.tensor
        def _(pe):
            pe.wait_ge(ident_set, 2)
            pe.wait_ge(vec_in, 16 * len(VECTORS))
            pe.transpose(DB[:, 0:len(VECTORS) * KT], vec_rows[:, :],
                         ident[0:len(VECTORS) * KT, 0:len(VECTORS) * KT]).then_inc(vec_t, 1)
            turner.turn(pe, [0, 1])
            pe.wait_ge(dec_in, 16)
            pe.wait_ge(vec_done, 1)
            pe.transpose(DB[:, 0:D // 8], decay_rows[:, :], ident[0:D // 8, 0:D // 8]).then_inc(dec_t, 1)
            pe.wait_ge(r_step, STEPS + 1)
            for q in range(NSB):
                if q >= 2:
                    pe.wait_ge(dec_done, q)
                for s in range(4):
                    mm = pe.transpose(SBK[q % 2][:, s * P:(s + 1) * P], state_cols[:, 4 * q + s, :], ident[:, :])
                mm.then_inc(st_done, 1)
            pe.wait_ge(q_step, 9)
            turner.turn(pe, [2])

        @block.vector
        def _(dve):
            a_count = [0]

            def chain(ins_):
                a_count[0] += 1
                ins_.then_inc(a_step, 1)
                dve.wait_ge(a_step, a_count[0])

            dve.wait_ge(a_exp_done, 1)
            dve.wait_ge(vec_done, 1)
            chain(nc.vector.tensor_scalar(a_den[:, :], a_exp[:, :], 1.0, None, ALU.add))
            chain(nc.vector.reciprocal(a_pow[:, 0, :], a_den[:, :]))
            for j in range(STEPS):
                chain(nc.vector.tensor_tensor(a_pow[:, j + 1, :], a_pow[:, j, :], a_pow[:, j, :], ALU.mult))
            turner.rest(dve, [0, 1])
            chain(nc.vector.tensor_tensor(cb[:, :, :], c_in[:, :, :], b_in[:, :, :], ALU.mult))
            chain(nc.vector.memset(kern[:, :, :], 0.0))
            chain(nc.vector.tensor_tensor(out_rows[:, :, 0:1], cb[:, :, :].rearrange("p t s -> p (t s)").unsqueeze(2),
                                          a_pow[:, 0, :].unsqueeze(2), ALU.mult))
            for j in range(STEPS):
                L = 1 << j
                chain(nc.vector.tensor_tensor(out_rows[:, :, L:2 * L], out_rows[:, :, 0:L],
                                              a_pow[:, j, :].unsqueeze(2).broadcast_to([P, GS, L]), ALU.mult))
            assert a_count[0] == ROW_STEPS
            quantise_weight(dve, w_nat[2])
            chain(nc.vector.tensor_reduce(kern[:, :, P:2 * P - 1],
                                          out_rows[:, :, 0:P - 1].rearrange("p (t s) m -> p t m s", t=KT),
                                          AX.X, ALU.add))
            chain(nc.vector.tensor_reduce(cb_sum[:, :], cb[:, :, :], AX.X, ALU.add))
            chain(nc.vector.tensor_tensor(kern[:, :, P - 1:P], cb_sum[:, :].unsqueeze(2), keep["cols"][:, 4 * KT:5 * KT].unsqueeze(2),
                                          ALU.add))
            assert a_count[0] == TABLE_STEPS

            turner.rest(dve, [2])


def phase_project(nc, sh, ins, scr, keep, banks):
    KT, D, GT, GN, NG = sh.KT, sh.D, sh.GT, sh.GN, sh.NG
    x_in = ins["L0_attn_x"].rearrange("b s d -> (b s) d").rearrange("(g t p) d -> g p t d", t=GT, p=P)
    z_out = scr["z"].rearrange("(g t p) d -> g p t d", t=GT, p=P)
    v_out = scr["v"].rearrange("(g t p) d -> g p t d", t=GT, p=P)
    with ExitStack() as ctx:
        def sb(name, shape, dt=F32):
            return ctx.enter_context(nc.sbuf_tensor(name, shape, dt))

        def sem(name):
            return keep["semaphores"].enter_context(nc.semaphore(name))

        w1, v1 = keep["w1"], keep["v1"]
        xg = [sb(f"b_xg{h}", [P, GT, D]) for h in range(2)]
        xn = sb("b_xn", [P, GT, D])
        xt = [sb(f"b_xt{h}", [P, 2, KT, GN], F32R) for h in range(2)]
        x1 = [sb(f"b_x1{h}", [P, KT, GN + 2]) for h in range(2)]
        conv = sb("b_conv", [P, KT, GN])
        conv_back = sb("b_conv_back", [P, KT, GN])
        zt = [sb(f"b_zt{h}", [P, GT, D]) for h in range(2)]
        vt = [sb(f"b_vt{h}", [P, GT, D]) for h in range(2)]
        stats = sb("b_stats", [P, GT, 6])
        moments = sb("b_moments", [P, GT, 2])
        var_eps = sb("b_var_eps", [P, GT])
        rstd = sb("b_rstd", [P, GT])
        bv1 = sb("b_bv1", [P, D])

        const_in = sem("b_const_in")
        x_in_sem = [sem(f"b_x_in{h}") for h in range(2)]
        st1, st2, st3 = sem("b_st1"), sem("b_st2"), sem("b_st3")
        rstd_done = sem("b_rstd_done")
        xn_done = sem("b_xn_done")
        t_full = sem("b_t_full")
        hi_done, lo_done = sem("b_hi_done"), sem("b_lo_done")
        x1_full, x1_done = sem("b_x1_full"), sem("b_x1_done")
        halo = sem("b_halo")
        mid_done, left_done, conv_done = sem("b_mid_done"), sem("b_left_done"), sem("b_conv_done")
        v_full, v_sum, v_done = sem("b_v_full"), sem("b_v_sum"), sem("b_v_done")
        z_full, z_done = sem("b_z_full"), sem("b_z_done")
        z_stored = [sem(f"b_z_stored{h}") for h in range(2)]
        v_stored = [sem(f"b_v_stored{h}") for h in range(2)]

        TB, XB, VB, ZB = banks[0:2], banks[2:4], banks[4:6], banks[6:8]
        ident = keep["ident"]
        block = ctx.enter_context(nc.Block("project"))

        def over_groups(eng, body):
            body(0, 0, True, False)
            body(1, 1, False, False)
            if NG > 4:
                with eng.Fori(1, NG // 2 - 1) as i:
                    body(i * 2, 0, False, False)
                    body(i * 2 + 1, 1, False, False)
            body(NG - 2, 0, False, False)
            body(NG - 1, 1, False, True)

        @block.sync
        def _(sp):
            for h in range(2):
                sp.dma_start(xg[h][:, :, :], x_in[h]).then_inc(x_in_sem[h], 16)

            def store_z(g, h):
                sp.wait_ge(z_done, GT * (g + 1))
                sp.dma_start(z_out[g], zt[h][:, :, :]).then_inc(z_stored[h], 16)

            def body(g, h, first, last):
                if not (isinstance(g, int) and g + 2 >= NG):
                    sp.wait_ge(xn_done, GT * (g + 1))
                    sp.dma_start(xg[h][:, :, :], x_in[g + 2]).then_inc(x_in_sem[h], 16)
                if not first:
                    store_z(g - 1, 1 - h)
                sp.wait_ge(v_done, GT * (g + 1))
                sp.dma_start(v_out[g], vt[h][:, :, :]).then_inc(v_stored[h], 16)

            over_groups(sp, body)
            store_z(NG - 1, 1)
            for h in range(2):
                sp.wait_ge(z_stored[h], 16 * NG // 2)
                sp.wait_ge(v_stored[h], 16 * NG // 2)

        @block.gpsimd
        def _(pool):
            def rstd_of(g):
                pool.wait_ge(st3, g + 1)
                nc.gpsimd.tensor_tensor(rstd[:, :], var_eps[:, :], keep["neg_half"][:, 0:GT], ALU.pow)\
                  .then_inc(rstd_done, 1)

            with pool.Fori(0, NG) as g:
                rstd_of(g)

        @block.vector
        def _(dve):
            def normalise(g, h):
                dve.wait_ge(x_in_sem[h], slot_dmas(g, h) + 16)
                for t in range(GT):
                    ins_ = nc.vector.bn_stats(stats[:, t, :], xg[h][:, t, :])
                ins_.then_inc(st1, 1)
                dve.wait_ge(st1, g + 1)
                nc.vector.memset(keep["beat"][:, :], 0.0)
                for t in range(GT):
                    ins_ = nc.vector.bn_aggr(moments[:, t, :], stats[:, t, :])
                ins_.then_inc(st2, 1)
                dve.wait_ge(st2, g + 1)
                nc.vector.tensor_scalar(var_eps[:, :], moments[:, :, 1], LN_EPS, None, ALU.add).then_inc(st3, 1)
                nc.vector.tensor_copy(keep["mean0"][:, bass.ds(g * GT, GT)], moments[:, :, 0])
                dve.wait_ge(rstd_done, g + 1)
                nc.vector.tensor_copy(keep["rstd0"][:, bass.ds(g * GT, GT)], rstd[:, :])
                if not (isinstance(g, int) and g == 0):
                    dve.wait_ge(t_full, KT * g)
                for t in range(GT):
                    ins_ = nc.vector.tensor_scalar(xn[:, t, :], xg[h][:, t, :], moments[:, t, 0:1], rstd[:, t:t + 1],
                                                   ALU.subtract, ALU.mult)
                    ins_.then_inc(xn_done, 1)

            def low_part(g, h, kt):
                dve.wait_ge(hi_done, KT * g + kt + 1)
                nc.vector.tensor_tensor(xt[h][:, 1, kt, :], TB[kt % 2][:, :], xt[h][:, 0, kt, :].bitcast(F32),
                                        ALU.subtract).then_inc(lo_done, 1)

            def left_terms(g, h):
                dve.wait_ge(halo, 2 * g + 1)
                for m in range(KT):
                    dve.wait_ge(mid_done, KT * g + m + 1)
                    nc.vector.scalar_tensor_tensor(conv[:, m, :], x1[h][:, m, 0:GN], keep["conv_col"][:, m, 0:1],
                                                   conv[:, m, :], ALU.mult, ALU.add).then_inc(left_done, 1)

            def right_terms(g, h):
                src = x1[h]
                for m in range(KT):
                    dve.wait_ge(left_done, KT * g + m + 1)
                    back = bass.AP(conv_back[:, :, :].tensor, m * GN + P - 1, [[KT * GN, P], [P, GT], [-1, P]])
                    nc.vector.scalar_tensor_tensor(back, src[:, m, 2:GN + 2].rearrange("p (t k) -> p t k", k=P),
                                                   keep["conv_col"][:, m, 2:3],
                                                   conv[:, m, :].rearrange("p (t k) -> p t k", k=P),
                                                   ALU.mult, ALU.add).then_inc(conv_done, 1)

            def body(g, h, first, last):
                if not last:
                    normalise(g + 1, 1 - h)
                if not first:
                    left_terms(g - 1, 1 - h)
                dve.wait_ge(x1_done, KT * (g + 1))
                if not first:
                    gate = keep["batch_mask"][:, bass.ds(g, 1)]
                    nc.vector.tensor_scalar(x1[h][:, :, 0:1], x1[1 - h][:, :, GN:GN + 1], gate, None,
                                            ALU.mult).then_inc(halo, 1)
                    nc.vector.tensor_scalar(x1[1 - h][:, :, GN + 1:GN + 2], x1[h][:, :, 1:2], gate, None,
                                            ALU.mult).then_inc(halo, 1)
                    dve.wait_ge(halo, 2 * g + 1)
                    right_terms(g - 1, 1 - h)
                for t in range(GT):
                    dve.wait_ge(v_full, GT * g + t + 1)
                    if not (first or (isinstance(g, int) and g == 1)) and t == 0:
                        dve.wait_ge(v_stored[h], slot_dmas(g, h))
                    nc.vector.tensor_tensor(vt[h][:, t, :], VB[t % 2][:, :], bv1[:, :], ALU.add)\
                      .then_inc(v_sum, 1)
                    if not last:
                        low_part(g + 1, 1 - h, t)

            nc.vector.memset(x1[0][:, :, 0:1], 0.0).then_inc(halo, 1)
            nc.vector.memset(x1[1][:, :, GN + 1:GN + 2], 0.0)
            normalise(0, 0)
            for kt in range(KT):
                low_part(0, 0, kt)
            dve.wait_ge(const_in, 16)
            over_groups(dve, body)
            left_terms(NG - 1, 1)
            nc.vector.memset(x1[1][:, :, GN + 1:GN + 2], 0.0).then_inc(halo, 1)
            dve.wait_ge(halo, 2 * NG)
            right_terms(NG - 1, 1)

        @block.scalar
        def _(act):
            load_row(act, bv1, ins["L0_attn_v1_b"]).then_inc(const_in, 16)

            def high_part(g, h, kt):
                act.wait_ge(t_full, KT * g + kt + 1)
                nc.scalar.activation(xt[h][:, 0, kt, :], TB[kt % 2][:, :], ACT.Copy).then_inc(hi_done, 1)

            def middle(g, h, m):
                if not (isinstance(g, int) and g == 0):
                    act.wait_ge(z_full, GT * g)
                nc.scalar.activation(conv[:, m, :], x1[h][:, m, 1:GN + 1], ACT.Copy,
                                     scale=keep["conv_col"][:, m, 1:2]).then_inc(mid_done, 1)

            def silu_z(g, h, t):
                act.wait_ge(z_full, GT * g + t + 1)
                if t == 0 and not (isinstance(g, int) and g < 2):
                    act.wait_ge(z_stored[h], slot_dmas(g, h))
                nc.scalar.activation(zt[h][:, t, :], ZB[t % 2][:, :], ACT.Silu).then_inc(z_done, 1)

            def body(g, h, first, last):
                for m in range(KT):
                    act.wait_ge(x1_full, KT * g + m + 1)
                    if m == 0 and not (isinstance(g, int) and g < 2):
                        act.wait_ge(conv_done, KT * (g - 1))
                    nc.scalar.activation(x1[h][:, m, 1:GN + 1], XB[m % 2][:, :], ACT.Identity,
                                         bias=keep["b1_col"][:, m:m + 1]).then_inc(x1_done, 1)
                    if not first:
                        if m == 0:
                            act.wait_ge(x1_done, KT * g)
                        middle(g - 1, 1 - h, m)
                for t in range(GT):
                    if not last:
                        high_part(g + 1, 1 - h, t)
                    act.wait_ge(v_sum, GT * g + t + 1)
                    nc.scalar.activation(vt[h][:, t, :], vt[h][:, t, :], ACT.Silu).then_inc(v_done, 1)
                    if not first and t:
                        silu_z(g - 1, 1 - h, t - 1)
                if not first:
                    silu_z(g - 1, 1 - h, GT - 1)

            for kt in range(KT):
                high_part(0, 0, kt)
            over_groups(act, body)
            act.wait_ge(x1_done, KT * NG)
            for m in range(KT):
                middle(NG - 1, 1, m)
            for t in range(GT):
                silu_z(NG - 1, 1, t)

        @block.tensor
        def _(pe):
            def turn_x(g, kt):
                if kt == 0:
                    pe.wait_ge(xn_done, GT * (g + 1))
                if not (isinstance(g, int) and g == 0 and kt < 2):
                    pe.wait_ge(lo_done, KT * g + kt - 1)
                for t in range(GT):
                    mm = pe.transpose(TB[kt % 2][:, t * P:(t + 1) * P], xn[:, t, kt * P:(kt + 1) * P], ident[:, :])
                mm.then_inc(t_full, 1)

            def turn_z(g, t):
                if t == 0:
                    pe.wait_ge(conv_done, KT * (g + 1))
                if not (isinstance(g, int) and g == 0 and t < 2):
                    pe.wait_ge(z_done, GT * g + t - 1)
                for m in range(KT):
                    mm = pe.transpose(ZB[t % 2][:, m * P:(m + 1) * P], conv_back[:, m, t * P:(t + 1) * P], ident[:, :])
                mm.then_inc(z_full, 1)

            def body(g, h, first, last):
                for m in range(KT):
                    if not (first and m < 2):
                        pe.wait_ge(x1_done, KT * g + m - 1)
                    for kt in range(KT):
                        if m == 0:
                            pe.wait_ge(lo_done, KT * g + kt + 1)
                        mm = split_products(pe, XB[m % 2][:, :],
                                            [w1[:, j, kt, m * P:(m + 1) * P] for j in range(2)],
                                            [xt[h][:, j, kt, :] for j in range(2)], kt == 0, kt == KT - 1)
                    mm.then_inc(x1_full, 1)
                for t in range(GT):
                    if not (first and t < 2):
                        pe.wait_ge(v_sum, GT * g + t - 1)
                    for kt in range(KT):
                        mm = split_products(pe, VB[t % 2][:, :],
                                            [xt[h][:, j, kt, t * P:(t + 1) * P] for j in range(2)],
                                            [v1[:, j, kt, :] for j in range(2)], kt == 0, kt == KT - 1)
                    mm.then_inc(v_full, 1)
                    if not last:
                        turn_x(g + 1, t)
                    if not first and t:
                        turn_z(g - 1, t - 1)
                if not first:
                    turn_z(g - 1, GT - 1)

            for kt in range(KT):
                turn_x(0, kt)
            over_groups(pe, body)
            for t in range(GT):
                turn_z(NG - 1, t)


def phase_state_space(nc, sh, ins, scr, keep, banks):
    D, T = sh.D, sh.T
    NCH = sh.NT
    OC = 8
    NO = P // OC
    NC = D // P
    U = 4
    PIECES = U
    COLS = OC * NCH
    assert NO // U == 4
    z_in = scr["z"].rearrange("(n m) d -> m n d", m=P)
    v_in = scr["v"].rearrange("(n m) d -> m n d", m=P)
    u_out = scr["u"].rearrange("(n m) d -> m n d", m=P)
    kern = scr["kern"]
    with ExitStack() as ctx:
        def sb(name, shape, dt=F32):
            return ctx.enter_context(nc.sbuf_tensor(name, shape, dt))

        def sem(name):
            return keep["semaphores"].enter_context(nc.semaphore(name))

        zg = [sb(f"c_zg{i}", [P, NCH, P]) for i in range(2)]
        vg = [sb(f"c_vg{i}", [P, NCH, P]) for i in range(2)]
        toep = [sb(f"c_toep{i}", [P, OC, P]) for i in range(U)]
        into = [sb(f"c_into{i}", [P, P]) for i in range(U)]
        outof = [sb(f"c_outof{i}", [P, P]) for i in range(U)]
        own_sum = [sb(f"c_own_sum{i}", [P, COLS + 1]) for i in range(2)]
        decay = [sb(f"c_decay{i}", [P, COLS]) for i in range(2)]
        state = [sb(f"c_state{i}", [P, COLS]) for i in range(2)]

        z_in_sem = [sem(f"c_z_in{i}") for i in range(2)]
        v_in_sem = [sem(f"c_v_in{i}") for i in range(2)]
        stream_in = [sem(f"c_stream_in{i}") for i in range(U)]
        s_full, s_done = sem("c_s_full"), sem("c_s_done")
        decay_done, state_done = sem("c_decay_done"), sem("c_state_done")
        y_full, u_done = sem("c_y_full"), sem("c_u_done")
        u_stored = [sem(f"c_u_stored{i}") for i in range(2)]
        zeroed = sem("c_zeroed")
        SB, YB = banks[0:2], banks[2:4]
        own = keep["own_mask"][:, :, :].rearrange("p c n -> p (c n)")
        carry = keep["carry_mask"][:, :, :].rearrange("p c n -> p (c n)")
        turner = WeightTurner(nc, ins, keep["weight_sems"], 3, [None] * 3, keep["stages"], banks[0:4], keep["ident"])
        block = ctx.enter_context(nc.Block("state_space"))

        def over_octets(eng, body):
            for cg in range(NC):
                if cg == 0:
                    for u in range(U):
                        body(0, 0, u, False)
                with eng.Fori(1 if cg == 0 else 0, NO // U - 1) as i:
                    for u in range(U):
                        body(cg, i * U, u, False)
                for u in range(U):
                    body(cg, NO - U, u, u == U - 1)

        @block.sync
        def _(sp):
            def load_stream(cg, j, u, after):
                o = j + (cg * NO + u)
                if after:
                    sp.wait_ge(y_full, o - U + 1)
                rows = bass.AP(kern.tensor, o * (OC * 2 * P), [[1, P], [2 * P, OC], [1, P]])
                sp.dma_start(toep[u][:, :, :], rows).then_inc(stream_in[u], 16)
                sp.dma_start(into[u][:, :], scr["state_in"][bass.ds(o, 1), :, :].rearrange("o k x -> k (o x)"))\
                  .then_inc(stream_in[u], 16)
                sp.dma_start(outof[u][:, :],
                             scr["state_out_rows"][bass.ds(o, 1), :, :].rearrange("o x m -> x (o m)"))\
                  .then_inc(stream_in[u], 16)

            def chunks(i):
                return slice(i * (NCH // PIECES), (i + 1) * (NCH // PIECES))

            def load_piece(cg, i, src, tiles, sems):
                sp.dma_start(tiles[cg % 2][:, chunks(i), :], src[:, chunks(i), cg * P:(cg + 1) * P])\
                  .then_inc(sems[cg % 2], 16)

            def store_piece(cg, i):
                if i == 0:
                    sp.wait_ge(u_done, (cg + 1) * NO)
                sp.dma_start(u_out[:, chunks(i), cg * P:(cg + 1) * P], vg[cg % 2][:, chunks(i), :])\
                  .then_inc(u_stored[cg % 2], 16)

            for i in range(PIECES):
                load_piece(0, i, z_in, zg, z_in_sem)
            for cg in range(NC):
                for q in range(NO // U):
                    for u in range(U):
                        load_stream(cg, q * U, u, cg > 0 or q > 0)
                        if cg == 0 and q == 0:
                            load_piece(0, u, v_in, vg, v_in_sem)
                        if cg >= 1 and q == 1:
                            store_piece(cg - 1, u)
                        if cg + 1 < NC and q == 2:
                            load_piece(cg + 1, u, z_in, zg, z_in_sem)
                        if cg + 1 < NC and q == 3:
                            if cg >= 1 and u == 0:
                                sp.wait_ge(u_stored[(cg - 1) % 2], 16 * PIECES * ((cg - 1) // 2 + 1))
                            load_piece(cg + 1, u, v_in, vg, v_in_sem)
                    if cg == 0 and q == 1:
                        turner.load(sp, [3, 4])
            for i in range(PIECES):
                store_piece(NC - 1, i)
            for i in range(2):
                sp.wait_ge(u_stored[i], 16 * PIECES * NC // 2)

        @block.scalar
        def _(act):
            def body(cg, j, u, last):
                o = j + (cg * NO + u)
                if not (cg == 0 and isinstance(o, int) and o < 2):
                    act.wait_ge(state_done, o - 1)
                nc.scalar.activation(decay[u % 2][:, :], carry, ACT.Copy,
                                     scale=keep["decay_col"][:, bass.ds(o, 1)]).then_inc(decay_done, 1)

            body(0, 0, 0, False)
            body(0, 0, 1, False)
            for u in (2, 3):
                body(0, 0, u, False)
            with act.Fori(1, NC * NO // U) as i:
                for u in range(U):
                    body(0, i * U, u, False)

        @block.vector
        def _(dve):
            def states(cg, j, u):
                o = j + (cg * NO + u)
                dve.wait_ge(s_full, o + 1)
                if not (isinstance(o, int) and o < 2):
                    dve.wait_ge(y_full, o - 1)
                nc.vector.tensor_tensor(own_sum[u % 2][:, 1:COLS + 1], SB[u % 2][:, 0:COLS], own, ALU.mult)\
                  .then_inc(s_done, 1)
                dve.wait_ge(s_done, o + 1)
                dve.wait_ge(decay_done, o + 1)
                nc.vector.tensor_tensor_scan(state[u % 2][:, :], decay[u % 2][:, :], own_sum[u % 2][:, 0:COLS],
                                             0.0, ALU.mult, ALU.add).then_inc(state_done, 1)

            def body(cg, j, u, last):
                if u + 1 < U:
                    states(cg, j, u + 1)
                elif not last:
                    states(cg, j + U, 0)
                elif cg + 1 < NC:
                    states(cg + 1, 0, 0)
                o = j + (cg * NO + u)
                if u == 0:
                    dve.wait_ge(v_in_sem[cg % 2], 16 * PIECES * (cg // 2 + 1))
                dve.wait_ge(y_full, o + 1)
                mine = vg[cg % 2][:, :, bass.ds(j * OC + u * OC, OC)].rearrange("p n c -> p c n")
                nc.vector.tensor_tensor(mine, YB[u % 2][:, 0:COLS].rearrange("p (c n) -> p c n", c=OC), mine,
                                        ALU.mult).then_inc(u_done, 1)

            for i in range(2):
                ins_ = nc.vector.memset(own_sum[i][:, 0:1], 0.0)
            ins_.then_inc(zeroed, 1)
            dve.wait_ge(zeroed, 1)
            states(0, 0, 0)
            over_octets(dve, body)

        @block.tensor
        def _(pe):
            def states(cg, j, u):
                o = j + (cg * NO + u)
                pe.wait_ge(stream_in[u], 48 * (cg * (NO // U)) + (j * (48 // U)) + 48)
                if not (isinstance(o, int) and o < 2):
                    pe.wait_ge(s_done, o - 1)
                zs = zg[cg % 2][:, :, bass.ds(j * OC + u * OC, OC)].rearrange("p n c -> p c n")
                pe.matmul(SB[u % 2][:, 0:COLS].rearrange("p (c n) -> p c n", c=OC), into[u][:, :], zs,
                          start=True, stop=True).then_inc(s_full, 1)

            def body(cg, j, u, last):
                if u + 1 < U:
                    states(cg, j, u + 1)
                elif not last:
                    states(cg, j + U, 0)
                elif cg + 1 < NC:
                    pe.wait_ge(z_in_sem[(cg + 1) % 2], 16 * PIECES * ((cg + 1) // 2 + 1))
                    states(cg + 1, 0, 0)
                o = j + (cg * NO + u)
                if not (isinstance(o, int) and o < 2):
                    pe.wait_ge(u_done, o - 1)
                for c in range(OC):
                    zc = zg[cg % 2][:, :, bass.ds(j * OC + (u * OC + c), 1)].rearrange("p n c -> p (n c)")
                    pe.matmul(YB[u % 2][:, c * NCH:(c + 1) * NCH], toep[u][:, c, :], zc,
                              start=(c == 0), stop=False, skip_group_check=True)
                pe.wait_ge(state_done, o + 1)
                pe.matmul(YB[u % 2][:, 0:COLS], outof[u][:, :], state[u % 2][:, :], start=False, stop=True,
                          skip_group_check=True).then_inc(y_full, 1)

            pe.wait_ge(z_in_sem[0], 16 * PIECES)
            states(0, 0, 0)
            over_octets(pe, body)


def phase_mix(nc, sh, ins, scr, keep, banks):
    KT, D, NTB, B = sh.KT, sh.D, sh.NTB, sh.B
    NBL = D // QBLOCK
    Q = 4
    assert NTB % Q == 0 and NTB >= 2 * Q
    x_in = ins["L0_attn_x"].rearrange("b s d -> (b s) d").rearrange("(n p) d -> p n d", p=P)
    u_in = scr["u"].rearrange("(n p) d -> p n d", p=P)
    x2_out = scr["x2"].rearrange("(n p) d -> p n d", p=P)
    with ExitStack() as ctx:
        def sb(name, shape, dt=F32):
            return ctx.enter_context(nc.sbuf_tensor(name, shape, dt))

        def sem(name):
            return keep["semaphores"].enter_context(nc.semaphore(name))

        w2 = sb("d_w2", [P, 2, KT, D], F32R)
        wf = sb("d_wf", [P, 2, KT, D], F32R)
        wk = sb("d_wk", [P, 2, KT, D], F32R)
        wv = sb("d_wv", [P, KT, D])
        xs = [sb(f"d_x{i}", [P, D]) for i in range(Q)]
        us = [sb(f"d_u{i}", [P, D]) for i in range(Q)]
        xb = [sb(f"d_xb{i}", [P, D]) for i in range(Q)]
        x2 = [sb(f"d_x2{i}", [P, D]) for i in range(Q)]
        xq = [sb(f"d_xq{i}", [P, D]) for i in range(2)]
        magic = sb("d_magic", [P, 2, D])
        q_max = sb("d_q_max", [P, NBL])
        q_inv = sb("d_q_inv", [P, NBL])
        q_scale = sb("d_q_scale", [P, 2, NBL])
        ut = [sb(f"d_ut{i}", [P, 2, KT, P], F32R) for i in range(2)]
        qt = [sb(f"d_qt{i}", [P, 2, KT, P], F32R) for i in range(2)]
        nt = [sb(f"d_nt{i}", [P, 2, KT, P], F32R) for i in range(2)]
        xn = [sb(f"d_xn{i}", [P, D]) for i in range(2)]
        nat = [sb(f"d_nat{i}", [P, 2, D], F32R) for i in range(Q)]
        kb = sb("d_kb", [P, D])
        kr = [sb(f"d_kr{i}", [P, D]) for i in range(2)]
        kh = [sb(f"d_kh{i}", [P, 2, D], F32R) for i in range(2)]
        kacc = sb("d_kacc", [P, D])
        stats = sb("d_stats", [P, 6])
        moments = [sb(f"d_moments{i}", [P, 2]) for i in range(2)]
        var_eps = sb("d_var_eps", [P, 1])
        rstd = [sb(f"d_rstd{i}", [P, 1]) for i in range(2)]
        res_bias = sb("d_res_bias", [P, D])
        ffn_bias = sb("d_ffn_bias", [P, D])
        bk = sb("d_bk", [P, D])
        zeros = sb("d_zeros", [P, D], F32R)
        ones = sb("d_ones", [P, 1])
        gt = keep["stages"][0]
        ksum_row = sb("d_ksum_row", [1, D])

        const_in = sem("d_const_in")
        bias_done = sem("d_bias_done")
        set_done = sem("d_set_done")
        x_ld = [sem(f"d_x_ld{i}") for i in range(Q)]
        u_ld = [sem(f"d_u_ld{i}") for i in range(Q)]
        x2_st = [sem(f"d_x2_st{i}") for i in range(Q)]
        prep = sem("d_prep")
        q_sub, q_done = sem("d_q_sub"), sem("d_q_done")
        xb_done = sem("d_xb_done")
        u_full, u_hi, u_lo = sem("d_u_full"), sem("d_u_hi"), sem("d_u_lo")
        q_full, q_hi, q_lo = sem("d_q_full"), sem("d_q_hi"), sem("d_q_lo")
        n_full, n_hi, n_lo = sem("d_n_full"), sem("d_n_hi"), sem("d_n_lo")
        x2_full, x2_done = sem("d_x2_full"), sem("d_x2_done")
        st1, st2, st3 = sem("d_st1"), sem("d_st2"), sem("d_st3")
        rstd_done = sem("d_rstd_done")
        xn_done = sem("d_xn_done")
        nat_hi, nat_lo = sem("d_nat_hi"), sem("d_nat_lo")
        k_full, kb_done = sem("d_k_full"), sem("d_kb_done")
        kr_done, k_hi, k_lo = sem("d_kr_done"), sem("d_k_hi"), sem("d_k_lo")
        kacc_done = sem("d_kacc_done")
        g_full, g_done = sem("d_g_full"), sem("d_g_done")
        ks_full, ks_done = sem("d_ks_full"), sem("d_ks_done")
        kv_full, kv_done = sem("d_kv_full"), sem("d_kv_done")

        BA, BB, BX, BK = banks[0:4]
        BG = banks[4:8]
        ident = keep["ident"]
        PREP = 8
        turner = WeightTurner(nc, ins, keep["weight_sems"], 3, [w2, wk, wv], keep["stages"], banks[0:4], ident)
        block = ctx.enter_context(nc.Block("mix"))

        def over_steps(eng, b, step):
            def one(n, q):
                known = isinstance(n, int)
                step(b, n, b * NTB + n, q,
                     one=not known or n < NTB,
                     two=not known or 1 <= n <= NTB,
                     three=not known or 2 <= n <= NTB + 1,
                     turn=not known or n + 1 < NTB,
                     prepare=not known or n + 2 < NTB,
                     load=not known or n + Q < NTB)

            for n in range(Q):
                one(n, n)
            if NTB > 2 * Q:
                with eng.Fori(1, NTB // Q - 1) as i:
                    for q in range(Q):
                        one(i * Q + q, q)
            for n in range(NTB - Q, NTB + 2):
                one(n, n % Q)

        @block.sync
        def _(sp):
            def load(N, q):
                if not (isinstance(N, int) and N < Q):
                    used = N - (Q - 1)
                    sp.wait_ge(prep, used * PREP)
                    sp.wait_ge(xb_done, used)
                sp.dma_start(xs[q][:, :], x_in[:, bass.ds(N, 1), :].rearrange("p n d -> p (n d)"))\
                  .then_inc(x_ld[q], 16)
                wait_reuse(sp, u_full, N, Q)
                sp.dma_start(us[q][:, :], u_in[:, bass.ds(N, 1), :].rearrange("p n d -> p (n d)"))\
                  .then_inc(u_ld[q], 16)

            def step(b, n, N, q, one, two, three, turn, prepare, load):
                if load:
                    load_tile(N + Q, q)
                if one:
                    sp.wait_ge(x2_done, N + 1)
                    sp.dma_start(x2_out[:, bass.ds(N, 1), :].rearrange("p n d -> p (n d)"), x2[q][:, :])\
                      .then_inc(x2_st[q], 16)

            load_tile = load
            for b in range(B):
                for n in range(Q):
                    load_tile(b * NTB + n, n)
                    if b == 0 and n == 1:
                        turner.load(sp, [5])
                if b == 0:
                    sp.dma_start(wf[:, :, :, :].bitcast(F32), scr["wf"]).then_inc(const_in, 16)
                over_steps(sp, b, step)
            for q in range(Q):
                sp.wait_ge(x2_st[q], 16 * B * NTB // Q)

        @block.gpsimd
        def _(pool):
            def prepare_tile(N, q):
                p = q % 2
                pool.wait_ge(prep, PREP * (N + 1))
                nc.gpsimd.tensor_tensor(xq[p][:, :], xq[p][:, :], magic[:, p, :], ALU.subtract).then_inc(q_sub, 1)
                pool.wait_ge(q_sub, N + 1)
                nc.gpsimd.tensor_tensor(xq[p][:, :].rearrange("p (b e) -> p b e", e=QBLOCK),
                                        xq[p][:, :].rearrange("p (b e) -> p b e", e=QBLOCK),
                                        q_scale[:, p, :].unsqueeze(2).broadcast_to([P, NBL, QBLOCK]),
                                        ALU.mult).then_inc(q_done, 1)

            def add_bias(N, q):
                pool.wait_ge(x_ld[q], (N - q) * (16 // Q) + 16)
                wait_reuse(pool, x2_done, N, Q)
                nc.gpsimd.tensor_tensor(xb[q][:, :], xs[q][:, :], res_bias[:, :], ALU.add).then_inc(xb_done, 1)

            def step(b, n, N, q, one, two, three, turn, prepare, load):
                if one:
                    p = q % 2
                    pool.wait_ge(st3, N + 1)
                    nc.gpsimd.tensor_tensor(rstd[p][:, :], var_eps[:, :], keep["neg_half"][:, 0:1], ALU.pow)\
                      .then_inc(rstd_done, 1)
                    pool.wait_ge(rstd_done, N + 1)
                    nc.gpsimd.tensor_copy(keep["rstd1"][:, bass.ds(N, 1)], rstd[p][:, :])
                    nc.gpsimd.tensor_copy(keep["mean1"][:, bass.ds(N, 1)], moments[p][:, 0:1])
                if turn:
                    add_bias(N + 1, (q + 1) % Q)
                if two:
                    pool.wait_ge(kr_done, N)
                    pool.wait_ge(kacc_done, N + b)
                    nc.gpsimd.tensor_tensor(kacc[:, :], kacc[:, :], kr[(q - 1) % 2][:, :], ALU.add)\
                      .then_inc(kacc_done, 1)
                if prepare:
                    prepare_tile(N + 2, (q + 2) % Q)

            nc.gpsimd.memset(ones[:, :], 1.0).then_inc(set_done, 1)
            nc.gpsimd.memset(zeros[:, :].bitcast(F32), 0.0).then_inc(set_done, 1)
            nc.gpsimd.memset(keep["kv"][:, :, :, :], 0.0).then_inc(set_done, 1)
            pool.wait_ge(const_in, 16 * 4)
            nc.gpsimd.tensor_tensor(res_bias[:, :], res_bias[:, :], ffn_bias[:, :], ALU.add).then_inc(bias_done, 1)
            pool.wait_ge(bias_done, 1)
            for b in range(B):
                if b:
                    pool.wait_ge(ks_full, b)
                nc.gpsimd.memset(kacc[:, :], 0.0).then_inc(kacc_done, 1)
                for n in range(2):
                    prepare_tile(b * NTB + n, n)
                add_bias(b * NTB, 0)
                over_steps(pool, b, step)

        @block.scalar
        def _(act):
            def step(b, n, N, q, one, two, three, turn, prepare, load):
                p = q % 2
                if two:
                    act.wait_ge(n_full, N)
                    nc.scalar.activation(nt[1 - p][:, 0, :, :], BA[:, :].rearrange("p (k t) -> p k t", k=KT),
                                         ACT.Copy).then_inc(n_hi, 1)
                if turn:
                    turned(N + 1, 1 - p)
                if one:
                    act.wait_ge(xn_done, N + 1)
                    nc.scalar.activation(nat[q][:, 0, :], xn[p][:, :], ACT.Copy).then_inc(nat_hi, 1)
                if two:
                    M = N - 1
                    act.wait_ge(kb_done, N)
                    if not (isinstance(M, int) and M < 2):
                        act.wait_ge(kacc_done, M - 1 + b)
                    nc.scalar.activation(kr[1 - p][:, :], kb[:, :], ACT.Relu).then_inc(kr_done, 1)
                    act.wait_ge(kr_done, N)
                    nc.scalar.activation(kh[1 - p][:, 0, :], kr[1 - p][:, :], ACT.Copy).then_inc(k_hi, 1)

            def turned(N, p):
                act.wait_ge(u_full, N + 1)
                nc.scalar.activation(ut[p][:, 0, :, :], BA[:, :].rearrange("p (k t) -> p k t", k=KT),
                                     ACT.Copy).then_inc(u_hi, 1)
                act.wait_ge(q_full, N + 1)
                nc.scalar.activation(qt[p][:, 0, :, :], BB[:, :].rearrange("p (k t) -> p k t", k=KT),
                                     ACT.Copy).then_inc(q_hi, 1)

            load_row(act, res_bias, ins["L0_attn_w2_b"]).then_inc(const_in, 16)
            load_row(act, ffn_bias, ins["L0_ffn_bias"]).then_inc(const_in, 16)
            load_row(act, bk, ins["L1_attn_bk"]).then_inc(const_in, 16)
            turner.round(act)
            for b in range(B):
                turned(b * NTB, 0)
                over_steps(act, b, step)
                act.wait_ge(g_full, b + 1)
                for c in range(KT):
                    nc.scalar.activation(gt[:, c, :], BG[c][:, :], ACT.Copy).then_inc(g_done, 1)

        @block.vector
        def _(dve):
            def low(bank, tile, hi_sem, lo_sem, n):
                dve.wait_ge(hi_sem, n)
                nc.vector.tensor_tensor(tile[:, 1, :, :], bank[:, :].rearrange("p (k t) -> p k t", k=KT),
                                        tile[:, 0, :, :].bitcast(F32), ALU.subtract).then_inc(lo_sem, 1)

            def prepare_tile(N, q, between=None):
                p = q % 2
                k = [0]

                def link(ins_):
                    k[0] += 1
                    ins_.then_inc(prep, 1)
                    if k[0] < PREP:
                        dve.wait_ge(prep, PREP * N + k[0])

                blocks = xq[p][:, :].rearrange("p (b e) -> p b e", e=QBLOCK)
                dve.wait_ge(x_ld[q], (N - q) * (16 // Q) + 16)
                wait_reuse(dve, q_full, N, 2)
                link(nc.vector.tensor_scalar(xq[p][:, :], xs[q][:, :], keep["mean0"][:, bass.ds(N, 1)],
                                             keep["rstd0"][:, bass.ds(N, 1)], ALU.subtract, ALU.mult))
                link(nc.vector.tensor_reduce(q_max[:, :], blocks, AX.X, ALU.max, apply_absolute_value=True))
                if between is not None:
                    between()
                link(nc.vector.tensor_scalar(q_scale[:, p, :], q_max[:, :], 1.0 / FP6_MAX, SCALE_EPS,
                                             ALU.mult, ALU.max))
                link(nc.vector.reciprocal(q_inv[:, :], q_scale[:, p, :]))
                link(nc.vector.tensor_tensor(blocks, blocks, q_inv[:, :].unsqueeze(2).broadcast_to([P, NBL, QBLOCK]),
                                             ALU.mult))
                link(nc.vector.tensor_scalar(magic[:, p, :].bitcast(U32), xq[p][:, :].bitcast(U32), EXPONENT_BITS,
                                             None, ALU.bitwise_and))
                link(nc.vector.tensor_scalar(magic[:, p, :], magic[:, p, :], 1.0, ROUND_MAGIC, ALU.max, ALU.mult))
                link(nc.vector.tensor_tensor(xq[p][:, :], xq[p][:, :], magic[:, p, :], ALU.add))

            def step(b, n, N, q, one, two, three, turn, prepare, load):
                p = q % 2
                if two:
                    low(BA, nt[1 - p], n_hi, n_lo, N)
                if one:
                    dve.wait_ge(x2_full, N + 1)
                    dve.wait_ge(xb_done, N + 1)
                    if not (isinstance(N, int) and N < Q):
                        dve.wait_ge(x2_st[q], (N - q) * (16 // Q))
                    nc.vector.tensor_tensor(x2[q][:, :], BX[:, :], xb[q][:, :], ALU.add).then_inc(x2_done, 1)
                    dve.wait_ge(x2_done, N + 1)
                    nc.vector.bn_stats(stats[:, :], x2[q][:, :]).then_inc(st1, 1)
                    dve.wait_ge(st1, N + 1)
                    nc.vector.memset(keep["beat"][:, :], 0.0)
                    nc.vector.bn_aggr(moments[p][:, :], stats[:, :]).then_inc(st2, 1)
                    dve.wait_ge(st2, N + 1)
                    nc.vector.tensor_scalar(var_eps[:, :], moments[p][:, 1:2], LN_EPS, None, ALU.add)\
                      .then_inc(st3, 1)
                if turn:
                    low(BA, ut[1 - p], u_hi, u_lo, N + 2)
                    low(BB, qt[1 - p], q_hi, q_lo, N + 2)
                if one:
                    dve.wait_ge(rstd_done, N + 1)
                    wait_reuse(dve, n_full, N, 2)
                    nc.vector.tensor_scalar(xn[p][:, :], x2[q][:, :], moments[p][:, 0:1], rstd[p][:, :],
                                            ALU.subtract, ALU.mult).then_inc(xn_done, 1)
                    dve.wait_ge(nat_hi, N + 1)
                    nc.vector.tensor_tensor(nat[q][:, 1, :], xn[p][:, :], nat[q][:, 0, :].bitcast(F32),
                                            ALU.subtract).then_inc(nat_lo, 1)
                if two:
                    dve.wait_ge(k_full, N)
                    wait_reuse(dve, kr_done, N - 1, 1)
                    nc.vector.tensor_tensor(kb[:, :], BK[:, :], bk[:, :], ALU.add).then_inc(kb_done, 1)

                def low_keys():
                    if two:
                        dve.wait_ge(k_hi, N)
                        nc.vector.tensor_tensor(kh[1 - p][:, 1, :], kr[1 - p][:, :],
                                                kh[1 - p][:, 0, :].bitcast(F32), ALU.subtract).then_inc(k_lo, 1)

                if prepare:
                    prepare_tile(N + 2, (q + 2) % Q, low_keys)
                else:
                    low_keys()

            turner.rest(dve, [3, 4])
            for b in range(B):
                for n in range(2):
                    prepare_tile(b * NTB + n, n)
                if b == 0:
                    turner.rest(dve, [5])
                    dve.wait_ge(const_in, 16 * 4)
                low(BA, ut[0], u_hi, u_lo, b * NTB + 1)
                low(BB, qt[0], q_hi, q_lo, b * NTB + 1)
                over_steps(dve, b, step)
                dve.wait_ge(ks_full, b + 1)
                nc.vector.tensor_copy(ksum_row[:, :], BA[0:1, :]).then_inc(ks_done, 1)
                dve.wait_ge(kv_full, b + 1)
                dve.wait_ge(set_done, 3)
                HD = D // HEADS
                for j in range(P // HD):
                    rows = slice(j * HD, (j + 1) * HD)
                    nc.vector.tensor_copy(keep["kv"][rows, b, :, j * HD:(j + 1) * HD],
                                          BX[rows, :].rearrange("p (t c) -> p t c", t=KT)[:, :, j * HD:(j + 1) * HD])
                    ins_ = nc.vector.tensor_copy(keep["kv"][rows, b, :, P + j:P + j + 1],
                                                 BB[rows, 0:KT].unsqueeze(2))
                ins_.then_inc(kv_done, 1)

        @block.tensor
        def _(pe):
            def turn_in(dst, src, s):
                for kt in range(KT):
                    mm = pe.transpose(dst[:, kt * P:(kt + 1) * P], src[:, kt * P:(kt + 1) * P], ident[:, :])
                mm.then_inc(s, 1)

            def turn_next(N, q, after):
                pe.wait_ge(u_ld[q], (N - q) * (16 // Q) + 16)
                if after:
                    pe.wait_ge(n_lo, N - 1)
                turn_in(BA, us[q], u_full)
                pe.wait_ge(q_done, N + 1)
                turn_in(BB, xq[q % 2], q_full)

            def parts(tile, kt):
                return [tile[:, j, kt, :] for j in range(2)]

            def step(b, n, N, q, one, two, three, turn, prepare, load):
                p = q % 2
                if one:
                    if not (isinstance(N, int) and N == 0):
                        pe.wait_ge(x2_done, N)
                    pe.wait_ge(u_lo, N + 1)
                    for kt in range(KT):
                        split_products(pe, BX[:, :], parts(ut[p], kt), parts(w2, kt), kt == 0, False)
                    pe.wait_ge(q_lo, N + 1)
                    for kt in range(KT):
                        mm = split_products(pe, BX[:, :], parts(qt[p], kt), parts(wf, kt), False, kt == KT - 1)
                    mm.then_inc(x2_full, 1)
                if two:
                    pe.wait_ge(xn_done, N)
                    turn_in(BA, xn[1 - p], n_full)
                if three:
                    M = N - 2
                    pe.wait_ge(nat_lo, M + 1)
                    pe.wait_ge(k_lo, M + 1)
                    s, r = nat[(q - 2) % Q], kh[p]
                    for c in range(KT):
                        cols = slice(c * P, (c + 1) * P)
                        for i, j in ((0, 0), (0, 1), (1, 0)):
                            mm = pe.matmul(BG[c][:, :], s[:, i, cols], r[:, j, :], start=False, stop=False,
                                           skip_group_check=True)
                if turn:
                    turn_next(N + 1, (q + 1) % Q, two)
                if two:
                    pe.wait_ge(n_lo, N)
                    wait_reuse(pe, kb_done, N - 1, 1)
                    for kt in range(KT):
                        mm = split_products(pe, BK[:, :], parts(nt[1 - p], kt), parts(wk, kt), kt == 0, kt == KT - 1)
                    mm.then_inc(k_full, 1)

            turner.turn(pe)
            turner.wait_all(pe)
            pe.wait_ge(set_done, 3)
            pe.wait_ge(const_in, 16 * 4)
            for b in range(B):
                if b:
                    pe.wait_ge(g_done, KT * b)
                    pe.wait_ge(kv_done, b)
                for c in range(KT):
                    pe.matmul(BG[c][:, :], zeros[:, 0:P], zeros[:, :], start=True, stop=False,
                              skip_group_check=True)
                turn_next(b * NTB, 0, False)
                over_steps(pe, b, step)
                pe.matmul(BG[0][:, :], zeros[:, 0:P], zeros[:, :], start=False, stop=True,
                          skip_group_check=True).then_inc(g_full, 1)
                pe.wait_ge(kacc_done, (b + 1) * NTB + b + 1)
                pe.matmul(BA[0:1, :], ones[:, :], kacc[:, :], start=True, stop=True)
                for t in range(KT):
                    mm = pe.matmul(BB[:, t:t + 1], kacc[:, t * P:(t + 1) * P], ones[:, :], start=True, stop=True)
                mm.then_inc(ks_full, 1)
                pe.wait_ge(g_done, KT * (b + 1))
                pe.wait_ge(ks_done, b + 1)
                for t in range(KT):
                    cols = slice(t * P, (t + 1) * P)
                    for c in range(KT):
                        pe.matmul(BX[:, cols], gt[:, c, cols], wv[:, c, cols], start=(c == 0), stop=False)
                    mm = pe.matmul(BX[:, cols], ksum_row[:, cols], keep["bv_row"][:, cols], start=False, stop=True)
                mm.then_inc(kv_full, 1)


def phase_second_layer(nc, sh, ins, scr, keep, banks):
    KT, D, GT, GN, NG, NGB, B = sh.KT, sh.D, sh.GT, sh.GN, sh.NG, sh.NGB, sh.B
    HD = D // HEADS
    HP = P // HD
    KVC = P + HP
    x2_in = scr["x2"].rearrange("(g t p) d -> p g t d", t=GT, p=P)
    out_d = scr["out"].rearrange("b s d -> (b s) d").rearrange("(g t p) d -> p g t d", t=GT, p=P)
    with ExitStack() as ctx:
        def sb(name, shape, dt=F32):
            return ctx.enter_context(nc.sbuf_tensor(name, shape, dt))

        def sem(name):
            return keep["semaphores"].enter_context(nc.semaphore(name))

        wk, wq, wr, wv = [sb(f"e_w{i}", [P, 2, KT, D], F32R) for i in range(4)]
        x2 = [sb(f"e_x2{i}", [P, GT, D]) for i in range(2)]
        xn = sb("e_xn", [P, GT, D])
        xt = sb("e_xt", [P, KT, GN + 1])
        ring = [sb(f"e_ring{i}", [P, 2, KT, GN], F32R) for i in range(2)]
        prev = [sb(f"e_prev{i}", [P, GN]) for i in range(2)]
        mixed = [sb(f"e_mixed{i}", [P, GN]) for i in range(2)]
        keys = sb("e_keys", [P, 2, KT, GN], F32R)
        kr = [sb(f"e_kr{i}", [P, GN]) for i in range(2)]
        kk = sb("e_kk", [P, GN])
        qt = sb("e_qt", [P, KT, GN])
        gate = sb("e_gate", [P, GT, D])
        ff = [sb(f"e_ff{i}", [P, D]) for i in range(2)]
        att = [sb(f"e_att{i}", [P, D]) for i in range(2)]
        y = [sb(f"e_y{i}", [P, D]) for i in range(GT)]
        den = sb("e_den", [P, 2, 2, HP])
        rden = sb("e_rden", [P, 2, 2, HP])
        stats = sb("e_stats", [P, 6])
        moments = [sb(f"e_moments{i}", [P, 2]) for i in range(2)]
        var_eps = sb("e_var_eps", [P, 1])
        rstd = [sb(f"e_rstd{i}", [P, 1]) for i in range(2)]
        gamma = sb("e_gamma", [P, D])
        beta = sb("e_beta", [P, D])
        rest_k = sb("e_rest_k", [P, KT])
        rest_r = sb("e_rest_r", [P, KT])
        shift1 = sb("e_shift1", [P, sh.NT])

        const_in = sem("e_const_in")
        x_ld = [sem(f"e_x_ld{i}") for i in range(2)]
        o_st = [sem(f"e_o_st{i}") for i in range(2)]
        set_done = sem("e_set_done")
        xn_done = sem("e_xn_done")
        t_full, xt_done = sem("e_t_full"), sem("e_xt_done")
        halo = sem("e_halo")
        prev_done, mix_done = sem("e_prev_done"), sem("e_mix_done")
        hi_done, lo_done = sem("e_hi_done"), sem("e_lo_done")
        k_full, kr_done, kk_done, kh_done, kl_done = [sem(f"e_k{i}") for i in range(5)]
        q_full, q_done = sem("e_q_full"), sem("e_q_done")
        r_full, gate_done = sem("e_r_full"), sem("e_gate_done")
        v_full, ff_done = sem("e_v_full"), sem("e_ff_done")
        c_full, den_done, rden_done, c_done = [sem(f"e_c{i}") for i in range(4)]
        again_done, base_done, sum_done = sem("e_again_done"), sem("e_base_done"), sem("e_sum_done")
        st1, st2, st3 = sem("e_st1"), sem("e_st2"), sem("e_st3")
        rstd_done, raw_in, scaled = sem("e_rstd_done"), sem("e_raw_in"), sem("e_scaled")
        shifted, out_done = sem("e_shifted"), sem("e_out_done")

        TB, KQB, RVB, CB = banks[0:2], banks[2:4], banks[4:6], banks[6:8]
        ident = keep["ident"]
        turner = WeightTurner(nc, ins, keep["weight_sems"], 6, [wk, wq, wr, wv], [qt, gate], banks[4:8], ident)
        block = ctx.enter_context(nc.Block("second_layer"))

        def over_groups(eng, body):
            for b in range(B):
                lo, hi = b * NGB // 2, (b + 1) * NGB // 2
                if b == 0:
                    body(0, 0, 0, True, False)
                    body(0, 1, 1, False, False)
                    lo += 1
                if b == B - 1:
                    hi -= 1
                if hi > lo:
                    with eng.Fori(lo, hi) as i:
                        body(b, i * 2, 0, False, False)
                        body(b, i * 2 + 1, 1, False, False)
                if b == B - 1:
                    body(b, NG - 2, 0, False, False)
                    body(b, NG - 1, 1, False, True)

        @block.sync
        def _(sp):
            def load(g, h):
                sp.dma_start(x2[h][:, :, :], x2_in[:, bass.ds(g, 1), :, :].rearrange("p g t d -> p (g t) d"))\
                  .then_inc(x_ld[h], 16)

            def body(b, g, h, first, last):
                sp.wait_ge(x_ld[h], slot_dmas(g, h) + 16)
                if not last:
                    if not first:
                        sp.wait_ge(o_st[1 - h], slot_dmas(g + 1, 1 - h))
                    load(g + 1, 1 - h)
                sp.wait_ge(out_done, GT * (g + 1))
                sp.wait_ge(again_done, GT * (g + 1))
                sp.dma_start(out_d[:, bass.ds(g, 1), :, :].rearrange("p g t d -> p (g t) d"), x2[h][:, :, :])\
                  .then_inc(o_st[h], 16)

            turner.load(sp, [6, 7])
            load(0, 0)
            turner.load(sp, [8, 9])
            over_groups(sp, body)
            for h in range(2):
                sp.wait_ge(o_st[h], 16 * NG // 2)

        @block.gpsimd
        def _(pool):
            def body(b, g, h, first, last):
                pool.wait_ge(x_ld[h], slot_dmas(g, h) + 16)
                if not (isinstance(g, int) and g < 2):
                    pool.wait_ge(o_st[h], slot_dmas(g, h))
                for t in range(GT):
                    pool.wait_ge(again_done, g * GT + (t + 1))
                    nc.gpsimd.tensor_tensor(x2[h][:, t, :], x2[h][:, t, :], beta[:, :], ALU.add)\
                      .then_inc(shifted, 1)
                for t in range(GT + 1):
                    if t < GT:
                        n = g * GT + t
                        pool.wait_ge(ff_done, n + 1)
                        pool.wait_ge(shifted, n + 1)
                        nc.gpsimd.tensor_tensor(x2[h][:, t, :], x2[h][:, t, :], ff[t % 2][:, :], ALU.add)\
                          .then_inc(base_done, 1)
                        pool.wait_ge(c_done, 2 * (n + 1))
                        nc.gpsimd.tensor_tensor(y[t][:, :], y[t][:, :], att[t % 2][:, :], ALU.add)\
                          .then_inc(sum_done, 1)
                    if 1 <= t <= GT:
                        n = g * GT + t - 1
                        pool.wait_ge(st3, n + 1)
                        nc.gpsimd.tensor_tensor(rstd[(t - 1) % 2][:, :], var_eps[:, :], keep["neg_half"][:, 0:1],
                                                ALU.pow).then_inc(rstd_done, 1)

            pool.wait_ge(const_in, 16 * 2)
            over_groups(pool, body)

        @block.scalar
        def _(act):
            def low_half(src, kt, slot):
                nc.scalar.activation(ring[slot][:, 0, kt, :], src, ACT.Copy).then_inc(hi_done, 1)

            def prev_term(g, m, kt, rest):
                n = g * 8 + (4 * m + kt)
                if m == 0:
                    act.wait_ge(xt_done, KT * g + kt + 1)
                    act.wait_ge(halo, g + 1)
                wait_reuse(act, mix_done, n, 2)
                nc.scalar.activation(prev[kt % 2][:, :], xt[:, kt, 0:GN], ACT.Copy, scale=rest[:, kt:kt + 1])\
                  .then_inc(prev_done, 1)

            def mix_high(g, slot, m, kt):
                act.wait_ge(mix_done, g * 8 + (4 * m + kt + 1))
                low_half(mixed[kt % 2][:, :], kt, slot)

            def turned(g, kt):
                act.wait_ge(t_full, KT * g + kt + 1)
                act.wait_ge(halo, g + 1)
                nc.scalar.activation(xt[:, kt, 1:GN + 1], TB[kt % 2][:, :], ACT.Copy).then_inc(xt_done, 1)

            def load_raw(g):
                act.dma_start(xn[:, :, :], x2_in[:, bass.ds(g, 1), :, :].rearrange("p g t d -> p (g t) d"))\
                   .then_inc(raw_in, 16)

            def again(g, h, t):
                n = g * GT + t
                if t == 0:
                    act.wait_ge(x_ld[h], slot_dmas(g, h) + 16)
                wait_reuse(act, out_done, n, GT)
                nc.scalar.activation(y[t][:, :], x2[h][:, t, :], ACT.Identity, scale=keep["rstd1"][:, bass.ds(n, 1)],
                                     bias=shift1[:, bass.ds(n, 1)]).then_inc(again_done, 1)

            def body(b, g, h, first, last):
                if not last:
                    load_raw(g + 1)
                for m in range(KT):
                    act.wait_ge(k_full, KT * g + m + 1)
                    wait_reuse(act, kk_done, g * KT + m, 2)
                    nc.scalar.activation(kr[m % 2][:, :], KQB[m % 2][:, :], ACT.Relu).then_inc(kr_done, 1)
                    act.wait_ge(kr_done, KT * g + m + 1)
                    nc.scalar.activation(keys[:, 0, m, :], kr[m % 2][:, :], ACT.Square).then_inc(kh_done, 1)
                    if m >= 2:
                        prev_term(g, 1, m - 2, rest_r)
                for m in range(KT):
                    mix_high(g, h, 1, m)
                    act.wait_ge(q_full, KT * g + m + 1)
                    if not (isinstance(g, int) and g == 0):
                        act.wait_ge(c_full, GT * g)
                    nc.scalar.activation(qt[:, m, :], KQB[m % 2][:, :], ACT.Relu,
                                         bias=keep["bq_col"][:, m:m + 1]).then_inc(q_done, 1)
                    again(g, h, m)
                    if m + 2 < KT:
                        prev_term(g, 1, m + 2, rest_r)
                for t in range(GT):
                    if not last:
                        turned(g + 1, t)
                        prev_term(g + 1, 0, t, rest_k)
                    act.wait_ge(r_full, GT * g + t + 1)
                    if not (isinstance(g, int) and g == 0):
                        act.wait_ge(ff_done, GT * g)
                    nc.scalar.activation(gate[:, t, :], RVB[t % 2][:, :], ACT.Sigmoid).then_inc(gate_done, 1)
                    if not last:
                        mix_high(g + 1, 1 - h, 0, t)
                if not last:
                    act.wait_ge(r_full, GT * (g + 1))
                    for kt in range(KT):
                        act.wait_ge(xt_done, KT * (g + 1) + kt + 1)
                        low_half(xt[:, kt, 1:GN + 1], kt, h)

            load_raw(0)
            load_row(act, gamma, ins["L1_attn_gamma"]).then_inc(const_in, 16)
            load_row(act, beta, ins["L1_attn_beta"]).then_inc(const_in, 16)
            act.wait_ge(set_done, 3)
            for kt in range(KT):
                turned(0, kt)
                prev_term(0, 0, kt, rest_k)
                mix_high(0, 0, 0, kt)
            for kt in range(KT):
                act.wait_ge(xt_done, kt + 1)
                low_half(xt[:, kt, 1:GN + 1], kt, 1)
            turner.round(act)
            over_groups(act, body)

        @block.vector
        def _(dve):
            def normalise(g):
                dve.wait_ge(raw_in, g * 16 + 16)
                for t in range(GT):
                    n = g * GT + t
                    nc.vector.tensor_scalar(xn[:, t, :], xn[:, t, :], keep["mean1"][:, bass.ds(n, 1)],
                                            keep["rstd1"][:, bass.ds(n, 1)], ALU.subtract, ALU.mult)\
                      .then_inc(xn_done, 1)

            def carry_over(g):
                nc.vector.tensor_scalar(xt[:, :, 0:1], xt[:, :, GN:GN + 1], keep["batch_mask"][:, bass.ds(g, 1)],
                                        None, ALU.mult).then_inc(halo, 1)

            def mix(g, slot, m, kt, mu):
                dve.wait_ge(prev_done, g * 8 + (4 * m + kt + 1))
                wait_reuse(dve, hi_done, g * 12 + (8 * m + kt), 2)
                nc.vector.scalar_tensor_tensor(mixed[kt % 2][:, :], xt[:, kt, 1:GN + 1], mu[:, kt:kt + 1],
                                               prev[kt % 2][:, :], ALU.mult, ALU.add).then_inc(mix_done, 1)
                dve.wait_ge(hi_done, g * 12 + (8 * m + kt + 1))
                rest(slot, kt, mixed[kt % 2][:, :])

            def rest(slot, kt, src):
                nc.vector.tensor_tensor(ring[slot][:, 1, kt, :], src, ring[slot][:, 0, kt, :].bitcast(F32),
                                        ALU.subtract).then_inc(lo_done, 1)

            def plain(g, slot, kt):
                dve.wait_ge(hi_done, g * 12 + (4 + kt + 1))
                rest(slot, kt, xt[:, kt, 1:GN + 1])

            def body(b, g, h, first, last):
                for m in range(KT):
                    dve.wait_ge(kr_done, KT * g + m + 1)
                    wait_reuse(dve, kl_done, g * KT + m, 1)
                    nc.vector.tensor_tensor(kk[:, :], kr[m % 2][:, :], kr[m % 2][:, :], ALU.mult).then_inc(kk_done, 1)
                    dve.wait_ge(kk_done, KT * g + m + 1)
                    dve.wait_ge(kh_done, KT * g + m + 1)
                    nc.vector.tensor_tensor(keys[:, 1, m, :], kk[:, :], keys[:, 0, m, :].bitcast(F32), ALU.subtract)\
                      .then_inc(kl_done, 1)
                for kt in range(KT):
                    mix(g, h, 1, kt, keep["mu_r_col"])
                if not last:
                    normalise(g + 1)
                    carry_over(g + 1)
                    for t in range(GT):
                        mix(g + 1, 1 - h, 0, t, keep["mu_k_col"])
                for t in range(GT + 2):
                    if t < GT:
                        tile_products(g, h, t)
                    if not last and t < GT:
                        plain(g + 1, h, t)
                    if 1 <= t <= GT:
                        tile_stats(g, t - 1)
                    if t >= 2:
                        tile_out(g, h, t - 2)

            def tile_products(g, h, t):
                n = g * GT + t
                dve.wait_ge(v_full, n + 1)
                dve.wait_ge(gate_done, n + 1)
                wait_reuse(dve, base_done, n, 2)
                nc.vector.tensor_tensor(ff[t % 2][:, :], RVB[t % 2][:, :], gate[:, t, :], ALU.mult)\
                  .then_inc(ff_done, 1)
                dve.wait_ge(c_full, n + 1)
                for c in range(2):
                    sums = CB[c][:, 0:2 * KVC].rearrange("p (a x) -> p a x", a=2)
                    nc.vector.tensor_scalar(den[:, c, :, :], sums[:, :, P:KVC], DENOM_EPS, None, ALU.max)\
                      .then_inc(den_done, 1)
                dve.wait_ge(den_done, 2 * (n + 1))
                nc.vector.reciprocal(rden[:, :, :, :].rearrange("p c a j -> p (c a j)"),
                                     den[:, :, :, :].rearrange("p c a j -> p (c a j)")).then_inc(rden_done, 1)
                dve.wait_ge(rden_done, n + 1)
                wait_reuse(dve, sum_done, n, 2)
                for c in range(2):
                    sums = CB[c][:, 0:2 * KVC].rearrange("p (a x) -> p a x", a=2)[:, :, 0:P]
                    nc.vector.tensor_tensor(
                        att[t % 2][:, c * 2 * P:(c + 1) * 2 * P].rearrange("p (a j d) -> p a j d", a=2, j=HP),
                        sums.rearrange("p a (j d) -> p a j d", j=HP),
                        rden[:, c, :, :].unsqueeze(3).broadcast_to([P, 2, HP, HD]), ALU.mult).then_inc(c_done, 1)

            def tile_stats(g, t):
                n = g * GT + t
                dve.wait_ge(sum_done, n + 1)
                nc.vector.bn_stats(stats[:, :], y[t][:, :]).then_inc(st1, 1)
                dve.wait_ge(st1, n + 1)
                nc.vector.memset(keep["beat"][:, :], 0.0)
                nc.vector.bn_aggr(moments[t % 2][:, :], stats[:, :]).then_inc(st2, 1)
                dve.wait_ge(st2, n + 1)
                wait_reuse(dve, rstd_done, n, 1)
                nc.vector.tensor_scalar(var_eps[:, :], moments[t % 2][:, 1:2], LN_EPS, None, ALU.add).then_inc(st3, 1)

                nc.vector.scalar_tensor_tensor(y[t][:, :], y[t][:, :], moments[t % 2][:, 0:1], gamma[:, :],
                                               ALU.subtract, ALU.mult).then_inc(scaled, 1)

            def tile_out(g, h, t):
                n = g * GT + t
                dve.wait_ge(rstd_done, n + 1)
                dve.wait_ge(base_done, n + 1)
                dve.wait_ge(scaled, n + 1)
                nc.vector.scalar_tensor_tensor(x2[h][:, t, :], y[t][:, :], rstd[t % 2][:, :], x2[h][:, t, :],
                                               ALU.mult, ALU.add).then_inc(out_done, 1)

            for tile, mu in ((rest_k, keep["mu_k_col"]), (rest_r, keep["mu_r_col"])):
                nc.vector.tensor_scalar(tile[:, :], mu, -1.0, 1.0, ALU.mult, ALU.add).then_inc(set_done, 1)
            nc.vector.scalar_tensor_tensor(shift1[:, :], keep["mean1"][:, :], -1.0, keep["rstd1"][:, :],
                                           ALU.mult, ALU.mult).then_inc(set_done, 1)
            nc.vector.memset(xt[:, :, 0:1], 0.0).then_inc(halo, 1)
            normalise(0)
            dve.wait_ge(const_in, 16 * 2)
            for kt in range(KT):
                mix(0, 0, 0, kt, keep["mu_k_col"])
            for kt in range(KT):
                plain(0, 1, kt)
            turner.rest(dve)
            over_groups(dve, body)

        @block.tensor
        def _(pe):
            def turn(g, kt):
                if kt == 0:
                    pe.wait_ge(xn_done, GT * (g + 1))
                wait_reuse(pe, xt_done, g * KT + kt, 2)
                for t in range(GT):
                    mm = pe.transpose(TB[kt % 2][:, t * P:(t + 1) * P], xn[:, t, kt * P:(kt + 1) * P], ident[:, :])
                mm.then_inc(t_full, 1)

            def channels_out(g, j, slot, w, done):
                for m in range(KT):
                    if m >= 2:
                        pe.wait_ge(kr_done if j == 0 else q_done, KT * g + m - 1)
                    elif j == 1:
                        pe.wait_ge(kr_done, KT * g + m + 3)
                    elif not (isinstance(g, int) and g == 0):
                        pe.wait_ge(q_done, KT * g + m - 1)
                    for kt in range(KT):
                        if m == 0:
                            pe.wait_ge(lo_done, 12 * g + (4 * j + kt + 1))
                        mm = split_products(pe, KQB[m % 2][:, :],
                                            [w[:, i, kt, m * P:(m + 1) * P] for i in range(2)],
                                            [ring[slot][:, i, kt, :] for i in range(2)], kt == 0, kt == KT - 1)
                    mm.then_inc(done, 1)

            def tokens_out(t, left, w):
                for kt in range(KT):
                    mm = split_products(pe, RVB[t % 2][:, :],
                                        [left[:, i, kt, t * P:(t + 1) * P] for i in range(2)],
                                        [w[:, i, kt, :] for i in range(2)], kt == 0, kt == KT - 1)
                return mm

            def body(b, g, h, first, last):
                channels_out(g, 0, h, wk, k_full)
                channels_out(g, 1, 1 - h, wq, q_full)
                for t in range(GT):
                    if t == 0:
                        pe.wait_ge(lo_done, 12 * g + 12)
                    if t < 2:
                        if not first:
                            pe.wait_ge(ff_done, GT * g - 1 + t)
                    else:
                        pe.wait_ge(gate_done, GT * g + t - 1)
                    tokens_out(t, ring[h], wr).then_inc(r_full, 1)
                    if not last:
                        turn(g + 1, t)
                for t in range(GT):
                    n = g * GT + t
                    if t < 2:
                        pe.wait_ge(gate_done, n + 3)
                    else:
                        pe.wait_ge(ff_done, n - 1)
                    if t == 0:
                        pe.wait_ge(kl_done, KT * (g + 1))
                    tokens_out(t, keys, wv).then_inc(v_full, 1)
                    if not (first and t == 0):
                        pe.wait_ge(c_done, 2 * n)
                    for a in range(KT):
                        mm = pe.matmul(CB[a // 2][:, a % 2 * KVC:(a % 2 + 1) * KVC], qt[:, a, t * P:(t + 1) * P],
                                       keep["kv"][:, b, a, :], start=True, stop=True)
                    mm.then_inc(c_full, 1)

            for kt in range(KT):
                turn(0, kt)
            turner.turn(pe)
            turner.wait_all(pe)
            over_groups(pe, body)


INPUTS = ["L0_attn_x", "L0_attn_w1_w", "L0_attn_w1_b", "L0_attn_v1_w", "L0_attn_v1_b", "L0_attn_w2_w",
          "L0_attn_w2_b", "L0_attn_conv_w", "L0_attn_A", "L0_attn_B_ssm", "L0_attn_C_ssm", "L0_attn_D_ssm",
          "L0_ffn_weight", "L0_ffn_bias", "L1_attn_Wq", "L1_attn_bq", "L1_attn_Wk", "L1_attn_bk",
          "L1_attn_Wv", "L1_attn_bv", "L1_attn_gamma", "L1_attn_beta", "L1_ffn_W_r", "L1_ffn_W_k",
          "L1_ffn_W_v", "L1_ffn_mu_r", "L1_ffn_mu_k"]


def two_layer_kernel(nc, ins, out):
    sh = Shapes(ins["L0_attn_x"])
    KT, D, T, NT = sh.KT, sh.D, sh.T, sh.NT
    NS = ins["L0_attn_A"].shape[1]
    OCT = D // 8

    def dram(name, shape, dt=F32):
        return nc.dram_tensor(name, shape, dt, kind="Internal").ap()

    scr = {
        "wf": dram("scr_wf", [P, 2, KT, D]),
        "kern": dram("scr_kern", [D, 2 * P]),
        "state_in": dram("scr_state_in", [OCT, P, P]),
        "state_out": dram("scr_state_out", [D, NS, P]),
        "decay": dram("scr_decay", [D, NS]),
        "z": dram("scr_z", [T, D]),
        "v": dram("scr_v", [T, D]),
        "u": dram("scr_u", [T, D]),
        "x2": dram("scr_x2", [T, D]),
    }
    scr["state_out_rows"] = scr["state_out"].rearrange("(o c) s m -> o (c s) m", c=8)
    with ExitStack() as ctx:
        def sb(name, shape, dt=F32):
            return ctx.enter_context(nc.sbuf_tensor(name, shape, dt))

        keep = {
            "semaphores": ctx,
            "ident": sb("ident", [P, P]),
            "own_mask": sb("own_mask", [P, 8, NT]),
            "carry_mask": sb("carry_mask", [P, 8, NT]),
            "batch_mask": sb("batch_mask", [P, sh.NG]),
            "beat": sb("beat", [P, 1]),
            "neg_half": sb("neg_half", [P, 8]),
            "decay_col": sb("decay_col", [P, OCT]),
            "cols": sb("cols", [P, len(VECTORS) * KT]),
            "conv_col": sb("conv_col", [P, KT, 3]),
            "bv_row": sb("bv_row", [1, D]),
            "mean0": sb("mean0", [P, NT]),
            "rstd0": sb("rstd0", [P, NT]),
            "mean1": sb("mean1", [P, NT]),
            "rstd1": sb("rstd1", [P, NT]),
            "kv": sb("kv", [P, sh.B, KT, P + 4]),
        }
        for i, name in enumerate(["b1_col", "bq_col", "mu_r_col", "mu_k_col"]):
            keep[name] = keep["cols"][:, i * KT:(i + 1) * KT]
        banks = [ctx.enter_context(nc.psum_tensor(f"bank{i}", [P, 512], F32)) for i in range(8)]
        keep["weight_sems"] = {
            "in": [ctx.enter_context(nc.semaphore(f"w_in{i}")) for i in range(3)],
            "turned": ctx.enter_context(nc.semaphore("w_turned")),
            "rounded": ctx.enter_context(nc.semaphore("w_rounded")),
            "rest": ctx.enter_context(nc.semaphore("w_rest")),
        }
        scr["out"] = out
        with ExitStack() as first:
            for name in ("w1", "v1"):
                keep[name] = first.enter_context(nc.sbuf_tensor(name, [P, 2, KT, D], F32R))
            phase_tables(nc, sh, ins, scr, keep, banks)
            phase_project(nc, sh, ins, scr, keep, banks)
        with ExitStack() as middle:
            keep["stages"] = [middle.enter_context(nc.sbuf_tensor(f"w_stage{i}", [P, KT, D], F32)) for i in range(2)]
            phase_state_space(nc, sh, ins, scr, keep, banks)
            phase_mix(nc, sh, ins, scr, keep, banks)
        phase_second_layer(nc, sh, ins, scr, keep, banks)


def kernel(**inputs):
    import numpy as np
    import concourse.bacc as bacc
    from concourse.bass_utils import run_bass_kernel_spmd

    nc = bacc.Bacc("TRN2", target_bir_lowering=False, num_devices=1)
    arrays, ins = {}, {}
    for name in INPUTS:
        a = np.ascontiguousarray(inputs[name])
        arrays[f"in_{name}"] = a
        ins[name] = nc.dram_tensor(f"in_{name}", a.shape, mybir.dt.from_np(a.dtype), kind="ExternalInput").ap()
    out = nc.dram_tensor("out", inputs["L0_attn_x"].shape, F32, kind="ExternalOutput").ap()
    two_layer_kernel(nc, ins, out)
    r = run_bass_kernel_spmd(nc, [arrays], core_ids=[0])
    return r.results[0]["out"]
```
